# Optimizing a Trainium2 kernel written in Bass

```python
import numpy as np
import jax
import jax.numpy as jnp

def _softmax(x, axis=-1):
    return jax.nn.softmax(x, axis=axis)

def _gelu(x):
    return jax.nn.gelu(x, approximate=True)

def _silu(x):
    return jax.nn.silu(x)

def _sigmoid(x):
    return jax.nn.sigmoid(x)

def _layernorm(x, axis=-1, eps=1e-05):
    m = jnp.mean(x, axis=axis, keepdims=True)
    v = jnp.var(x, axis=axis, keepdims=True)
    return (x - m) / jnp.sqrt(v + eps)

def _scatter_add(tgt, idx, src, axis=0):
    return tgt.at[idx].add(src)

def _segment_sum(src, seg, n):
    return jax.ops.segment_sum(src, seg, n)
kernel_name = 'mk_conv_seq_d1_conv_nhwc128_r2_e515cf'

def setup_inputs(seed: int=0):
    np.random.seed(seed)
    _w = jnp.asarray

    def _rec_inputs():
        import jax
        import jax.numpy as jnp
        _gk = jax.random.key(seed)
        x = -0.0002928 + 1 * jax.random.normal(jax.random.fold_in(_gk, 1), (8, 32, 32, 64), jnp.float32)
        return x
    x = _rec_inputs()

    def _L0_conv_setup():
        import jax, jax.numpy as jnp
        import numpy as np
        GROUPS = 8
        EPS = 1e-05

        def group_norm(x, gamma, beta):
            B, H, W, C = x.shape
            g = GROUPS
            xg = x.reshape(B, H, W, g, C // g)
            mean = jnp.mean(xg, axis=(1, 2, 4), keepdims=True)
            var = jnp.var(xg, axis=(1, 2, 4), keepdims=True)
            xg = (xg - mean) / jnp.sqrt(var + EPS)
            return gamma * xg.reshape(B, H, W, C) + beta
        key = jax.random.key(seed)
        ks = jax.random.split(key, 6)
        B, H, W, C = (8, 32, 32, 64)
        s = 1.0 / np.sqrt(C)
        return {'x': jax.random.normal(ks[0], (B, H, W, C), jnp.float32), 'gamma': jnp.ones((C,), jnp.float32), 'beta': jnp.zeros((C,), jnp.float32), 'wq': jax.random.normal(ks[1], (C, C), jnp.float32) * s, 'bq': jnp.zeros((C,), jnp.float32), 'wk': jax.random.normal(ks[2], (C, C), jnp.float32) * s, 'bk': jnp.zeros((C,), jnp.float32), 'wv': jax.random.normal(ks[3], (C, C), jnp.float32) * s, 'bv': jnp.zeros((C,), jnp.float32), 'wp': jax.random.normal(ks[4], (C, C), jnp.float32) * s, 'bp': jnp.zeros((C,), jnp.float32)}
    _L0_conv_all = _L0_conv_setup()
    _L0_conv_in = {k: v for k, v in _L0_conv_all.items() if k in ('gamma', 'beta', 'wq', 'bq', 'wk', 'bk', 'wv', 'bv', 'wp', 'bp')}
    del _L0_conv_all
    return {'x': x, 'L0_conv_gamma': _L0_conv_in['gamma'], 'L0_conv_beta': _L0_conv_in['beta'], 'L0_conv_wq': _L0_conv_in['wq'], 'L0_conv_bq': _L0_conv_in['bq'], 'L0_conv_wk': _L0_conv_in['wk'], 'L0_conv_bk': _L0_conv_in['bk'], 'L0_conv_wv': _L0_conv_in['wv'], 'L0_conv_bv': _L0_conv_in['bv'], 'L0_conv_wp': _L0_conv_in['wp'], 'L0_conv_bp': _L0_conv_in['bp']}

def reference(x, L0_conv_gamma, L0_conv_beta, L0_conv_wq, L0_conv_bq, L0_conv_wk, L0_conv_bk, L0_conv_wv, L0_conv_bv, L0_conv_wp, L0_conv_bp):
    import jax
    import jax.numpy as jnp

    def _L0_conv_ref(x, gamma, beta, wq, bq, wk, bk, wv, bv, wp, bp):
        import jax, jax.numpy as jnp
        import numpy as np
        GROUPS = 8
        EPS = 1e-05

        def group_norm(x, gamma, beta):
            B, H, W, C = x.shape
            g = GROUPS
            xg = x.reshape(B, H, W, g, C // g)
            mean = jnp.mean(xg, axis=(1, 2, 4), keepdims=True)
            var = jnp.var(xg, axis=(1, 2, 4), keepdims=True)
            xg = (xg - mean) / jnp.sqrt(var + EPS)
            return gamma * xg.reshape(B, H, W, C) + beta
        B, H, W, C = x.shape
        scale = jnp.asarray(C, jnp.float32) ** (-0.5)
        xn = group_norm(x, gamma, beta)
        N = H * W
        xf = xn.reshape(B, N, C)
        q = xf @ wq + bq
        k = xf @ wk + bk
        v = xf @ wv + bv
        attn = jnp.einsum('bnc,bmc->bnm', q, k) * scale
        attn = jax.nn.softmax(attn, axis=-1)
        out = jnp.einsum('bnm,bmc->bnc', attn, v)
        out = out @ wp + bp
        return (xf + out).reshape(B, H, W, C)

    def _gn(v, G=32, eps=1e-05):
        B_, H_, W_, C_ = v.shape
        g = v.reshape(B_, H_, W_, G, C_ // G)
        m = jnp.mean(g, axis=(1, 2, 4), keepdims=True)
        s = jnp.var(g, axis=(1, 2, 4), keepdims=True)
        return ((g - m) / jnp.sqrt(s + eps)).reshape(v.shape)

    def _ln_c(v, eps=1e-06):
        m = jnp.mean(v, axis=-1, keepdims=True)
        s = jnp.var(v, axis=-1, keepdims=True)
        return (v - m) / jnp.sqrt(s + eps)

    def _ln_t(v, eps=1e-05):
        m = jnp.mean(v, axis=-1, keepdims=True)
        s = jnp.var(v, axis=-1, keepdims=True)
        return (v - m) / jnp.sqrt(s + eps)

    def _to_tokens(v):
        B_, H_, W_, C_ = v.shape
        return v.reshape(B_, H_ * W_, C_)

    def _from_tokens(t, like):
        return t.reshape(like.shape)
    x = _L0_conv_ref(x, L0_conv_gamma, L0_conv_beta, L0_conv_wq, L0_conv_bq, L0_conv_wk, L0_conv_bk, L0_conv_wv, L0_conv_bv, L0_conv_wp, L0_conv_bp)
    return x

_drawn_inputs = setup_inputs


def setup_inputs(seed=0):
    import zlib

    import numpy as np

    out = dict(_drawn_inputs(seed))
    spreads = {'L0_conv_gamma': (1.0, 0.2),
     'L0_conv_beta': (0.0, 0.1),
     'L0_conv_bq': (0.0, 0.562),
     'L0_conv_bk': (0.0, 0.8),
     'L0_conv_bv': (0.0, 0.1),
     'L0_conv_bp': (0.0, 0.1)}
    factors = {}
    for name, (base, spread) in spreads.items():
        noise = np.random.default_rng([zlib.crc32(name.encode()), seed]).standard_normal(out[name].shape)
        drawn = base * np.exp(spread * noise) if base else spread * noise
        out[name] = jnp.asarray(drawn.astype(out[name].dtype))
    for name, factor in factors.items():
        out[name] = (out[name] * factor).astype(out[name].dtype)
    return out
```

```python
import numpy as np
import concourse.bass as bass
from concourse import mybir
from contextlib import ExitStack



def attention_block(nc, x, gamma, beta, wq, bq, wk, bk, wv, bv, wp, bp, identity_in, group_mean_in, out):
    fp32 = mybir.dt.float32
    fp32r = mybir.dt.float32r
    ALU = mybir.AluOpType
    ACT = mybir.ActivationFunctionType
    AX = mybir.AxisListType

    BATCH, HEIGHT, WIDTH, C = x.shape
    PIXELS = HEIGHT * WIDTH
    P = 128
    T = PIXELS // P
    HALF = PIXELS // 2
    PAIRS = T // 2
    SCALE = float(C) ** -0.5
    EPS = 1e-5
    E_RING = 4
    DMA = 16
    FILLS = 10
    MOVES = 6

    x_nat = x.rearrange("b h w c -> b (h w) c").rearrange("b (p t) c -> b p (t c)", p=P)
    out_nat = out.rearrange("b h w c -> b (h w) c").rearrange("b (p t) c -> b p (t c)", p=P)

    def column(v):
        return v.rearrange("(c o) -> c o", o=1)

    def row(v):
        return v.rearrange("(o c) -> o c", o=1)

    ctx = ExitStack()
    with ctx:
        def sb(name, shape, dt=fp32):
            return ctx.enter_context(nc.sbuf_tensor(name, shape, dt))

        def ps(name, shape):
            return ctx.enter_context(nc.psum_tensor(name, shape, fp32))

        def sem(name):
            return ctx.enter_context(nc.semaphore(name))

        identity = sb("identity", [P, P])
        group_mean = sb("group_mean", [P, P])
        ones = sb("ones", [P, P])
        w_qk = sb("w_qk", [P, P])
        w_v2 = sb("w_v2", [P, P])
        w_p2 = sb("w_p2", [P, P])
        gamma_col = sb("gamma_col", [P, 1])
        beta_col = sb("beta_col", [C, 1])
        beta_wide = sb("beta_wide", [C, P])
        bias_qk_in = sb("bias_qk_in", [P, 1])
        bias_qk = sb("bias_qk", [P, 1])
        row_bv = sb("row_bv", [1, C])
        row_bp = sb("row_bp", [1, C])
        row_beta = sb("row_beta", [1, C])
        bias_v = sb("bias_v", [P, C])
        bias_out = sb("bias_out", [P, C])
        x_in = [sb(f"x_in{u}", [P, T * C]) for u in range(2)]
        x_T = sb("x_T", [P, HALF])
        xn_T = sb("xn_T", [P, HALF])
        bn6 = sb("bn6", [P, 6])
        part_means = bn6[:, 1:6:3]
        part_moments = bn6[:, 2:6:3]
        group_mean_of = sb("group_mean_of", [P, 1])
        mean_diff = sb("mean_diff", [P, 2])
        var_terms = sb("var_terms", [P, 4])
        var_eps = sb("var_eps", [P, 1])
        minus_half = sb("minus_half", [P, 1])
        rstd = sb("rstd", [P, 1])
        gain = sb("gain", [P, 1])
        diag = sb("diag", [C, 2, C])
        residual = sb("residual", [P, BATCH * T * C])
        centred = sb("centred", [P, T * C])
        scaled = sb("scaled", [P, T * C])
        hi = sb("hi", [P, PIXELS], fp32r)
        lo = sb("lo", [P, PIXELS], fp32r)
        queries_hi = [sb(f"queries_hi{u}", [P, PIXELS], fp32r) for u in range(2)]
        queries_lo = [sb(f"queries_lo{u}", [P, PIXELS], fp32r) for u in range(2)]
        keys_hilo = [sb(f"keys_hilo{u}", [P, PIXELS], fp32r) for u in range(2)]
        keys_guard = [sb(f"keys_guard{u}", [P, PIXELS], fp32r) for u in range(2)]
        values = [sb(f"values{u}", [P, T * C]) for u in range(2)]
        chunk_max = sb("chunk_max", [P, T])
        max_T = sb("max_T", [T, P], fp32r)
        probs = [sb(f"probs{k}", [P, PIXELS]) for k in range(E_RING)]
        prob_sum = [sb(f"prob_sum{u}", [P, PIXELS]) for u in range(2)]
        attn_T = sb("attn_T", [P, HALF])
        inv_den = sb("inv_den", [P, T])
        y_mul = sb("y_mul", [P, T * C])
        y_out = [sb(f"y_out{u}", [P, T * C]) for u in range(2)]

        scores = ps("scores", [P, PIXELS])
        wide = [ps(f"wide{k}", [P, PIXELS]) for k in range(2)]
        attn = ps("attn", [P, HALF])
        misc = ps("misc", [P, HALF])

        weights_in = sem("weights_in")
        x_loaded = [sem(f"x_loaded{u}") for u in range(2)]
        stacks_moved = sem("stacks_moved")
        max_placed = sem("max_placed")
        y_freed = [sem(f"y_freed{u}") for u in range(2)]
        fills_done = sem("fills_done")
        beta_wide_done = sem("beta_wide_done")
        biases_made = sem("biases_made")
        biases_done = sem("biases_done")
        xT_made = sem("xT_made")
        xT_copied = sem("xT_copied")
        bn_done = sem("bn_done")
        moments_done = sem("moments_done")
        mean_made = sem("mean_made")
        mean_done = sem("mean_done")
        diff_done = sem("diff_done")
        diff2_done = sem("diff2_done")
        var_made = sem("var_made")
        var_done = sem("var_done")
        rstd_done = sem("rstd_done")
        gain_done = sem("gain_done")
        xnT_done = sem("xnT_done")
        diag_done = sem("diag_done")
        coef_made = sem("coef_made")
        centred_done = sem("centred_done")
        scaled_done = sem("scaled_done")
        residual_done = sem("residual_done")
        qk_made = sem("qk_made")
        hi_done = sem("hi_done")
        lo_done = sem("lo_done")
        v_made = sem("v_made")
        values_done = sem("values_done")
        wide_made = sem("wide_made")
        max_done = sem("max_done")
        maxT_made = sem("maxT_made")
        maxT_done = sem("maxT_done")
        scores_made = sem("scores_made")
        exp_done = sem("exp_done")
        pv_done = sem("pv_done")
        sum_done = sem("sum_done")
        attnT_done = sem("attnT_done")
        y_made = sem("y_made")
        sum_freed = sem("sum_freed")
        inv_done = sem("inv_done")
        y_mul_done = sem("y_mul_done")
        y_done = sem("y_done")

        def per_channel(ap):
            return ap.unsqueeze(1).to_broadcast([P, T, C])

        def pixels(ap):
            return ap.rearrange("p (t c) -> p t c", t=T)

        FIRST, LOOP_FROM, LOOP_TO = 0, 1, BATCH - 3

        def all_images(eng, prologue, image):
            prologue()
            image(FIRST, FIRST % 2, prior=False, nxt=True, after=True)
            with eng.Fori(LOOP_FROM, LOOP_TO, 2) as b:
                image(b, LOOP_FROM % 2, prior=True, nxt=True, after=True)
                image(b + 1, (LOOP_FROM + 1) % 2, prior=True, nxt=True, after=True)
            image(BATCH - 3, (BATCH - 3) % 2, prior=True, nxt=True, after=True)
            image(BATCH - 2, (BATCH - 2) % 2, prior=True, nxt=True, after=False)
            image(BATCH - 1, (BATCH - 1) % 2, prior=True, nxt=False, after=False)

        block = ctx.enter_context(nc.Block())

        @block.sync
        def _(sp):
            def load_x(b, u):
                sp.dma_start(x_in[u][:, :], x_nat[bass.ds(b, 1)].rearrange("o p f -> (o p) f")).then_inc(x_loaded[u], DMA)

            def stack(p, u):
                sp.wait_ge(hi_done, 2 * p + 2)
                sp.dma_start(queries_hi[u][0:C, :].bitcast(fp32), hi[0:C, :].bitcast(fp32)).then_inc(stacks_moved, DMA)
                sp.dma_start(queries_hi[u][C:P, :].bitcast(fp32), hi[0:C, :].bitcast(fp32)).then_inc(stacks_moved, DMA)
                sp.dma_start(keys_hilo[u][0:C, :].bitcast(fp32), hi[C:P, :].bitcast(fp32)).then_inc(stacks_moved, DMA)
                sp.wait_ge(lo_done, 2 * p + 2)
                sp.dma_start(keys_hilo[u][C:P, :].bitcast(fp32), lo[C:P, :].bitcast(fp32)).then_inc(stacks_moved, DMA)
                sp.dma_start(keys_guard[u][0:C, :].bitcast(fp32), hi[C:P, :].bitcast(fp32)).then_inc(stacks_moved, DMA)
                sp.dma_start(queries_lo[u][0:C, :].bitcast(fp32), lo[0:C, :].bitcast(fp32)).then_inc(stacks_moved, DMA)

            def place_max(p, u):
                sp.wait_ge(maxT_done, p + 1)
                sp.dma_start(queries_lo[u][C:C + 1, :].bitcast(fp32).rearrange("o (t q) -> o t q", t=T),
                             max_T[:, :].bitcast(fp32)).then_inc(max_placed, DMA)

            def store(b, u):
                sp.wait_ge(y_done, b + 1)
                sp.dma_start(out_nat[bass.ds(b, 1)].rearrange("o p f -> (o p) f"), y_out[u][:, :]).then_inc(y_freed[u], DMA)

            def prologue():
                load_x(0, 0)
                sp.dma_start(identity[:, :], identity_in).then_inc(weights_in, DMA)
                sp.dma_start(group_mean[:, :], group_mean_in).then_inc(weights_in, DMA)
                load_x(1, 1)
                sp.wait_ge(fills_done, FILLS)
                stack(0, 0)
                place_max(0, 0)

            def image(b, u, prior, nxt, after):
                if after:
                    sp.wait_ge(centred_done, b + 1)
                    load_x(b + 2, u)
                if nxt:
                    stack(b + 1, 1 - u)
                if prior:
                    store(b - 1, 1 - u)
                if nxt:
                    place_max(b + 1, 1 - u)

            all_images(sp, prologue, image)
            store(BATCH - 1, (BATCH - 1) % 2)
            for u in range(2):
                sp.wait_ge(y_freed[u], DMA * (BATCH // 2 + 1))

        @block.gpsimd
        def _(pool):
            def rstd_of(s):
                pool.wait_ge(var_done, s + 1)
                if not isinstance(s, int) or s > 0:
                    pool.wait_ge(gain_done, s)
                nc.gpsimd.tensor_tensor(rstd[:, :], var_eps[:, :], minus_half[:, :], ALU.pow).then_inc(rstd_done, 1)

            def prologue():
                pool.wait_ge(fills_done, FILLS)
                rstd_of(0)
                rstd_of(1)

            def image(b, u, prior, nxt, after):
                for i in range(1, T):
                    pool.wait_ge(exp_done, 2 * T * b + 2 * i + 2)
                    if i == 1:
                        pool.wait_ge(sum_freed, b + 1)
                        first = probs[0]
                    else:
                        pool.wait_ge(sum_done, (T - 1) * b + i - 1)
                        first = prob_sum[u]
                    nc.gpsimd.tensor_tensor(prob_sum[u][:, :], first[:, :], probs[i % E_RING][:, :],
                                            ALU.add).then_inc(sum_done, 1)
                    if i == 5 and after:
                        rstd_of(b + 2)

            all_images(pool, prologue, image)

        @block.scalar
        def _(act):
            def copy_xT(s):
                act.wait_ge(xT_made, s + 1)
                if not isinstance(s, int) or s > 0:
                    act.wait_ge(xnT_done, s)
                nc.scalar.copy(x_T[:, :], misc[:, :]).then_inc(xT_copied, 1)

            def split_hi(p):
                for h in range(2):
                    act.wait_ge(qk_made, 2 * p + h + 1)
                    if h == 0 and (not isinstance(p, int) or p > 0):
                        act.wait_ge(stacks_moved, MOVES * DMA * p)
                    nc.scalar.activation(hi[:, h * HALF:(h + 1) * HALF], wide[0][:, h * HALF:(h + 1) * HALF],
                                         ACT.Identity, bias=bias_qk[:, 0:1]).then_inc(hi_done, 1)

            def copy_attn(b):
                act.wait_ge(pv_done, T * b + T)
                if not isinstance(b, int) or b > 0:
                    act.wait_ge(y_made, b)
                nc.scalar.copy(attn_T[:, :], attn[:, :]).then_inc(attnT_done, 1)

            def prologue():
                act.dma_start(w_qk[0:C, 0:C], wq).then_inc(weights_in, DMA)
                act.dma_start(w_qk[0:C, C:P], wk).then_inc(weights_in, DMA)
                act.dma_start(w_qk[C:P, 0:C], wq).then_inc(weights_in, DMA)
                act.dma_start(w_qk[C:P, C:P], wk).then_inc(weights_in, DMA)
                act.dma_start(beta_col[:, :], column(beta)).then_inc(weights_in, DMA)
                act.dma_start(gamma_col[0:C, :], column(gamma)).then_inc(weights_in, DMA)
                act.dma_start(gamma_col[C:P, :], column(gamma)).then_inc(weights_in, DMA)
                act.dma_start(bias_qk_in[0:C, :], column(bq)).then_inc(weights_in, DMA)
                act.dma_start(bias_qk_in[C:P, :], column(bk)).then_inc(weights_in, DMA)
                act.wait_ge(fills_done, FILLS)
                act.dma_start(w_v2[0:C, 0:C], wv).then_inc(weights_in, DMA)
                act.dma_start(w_v2[C:P, C:P], wv).then_inc(weights_in, DMA)
                act.dma_start(w_p2[0:C, 0:C], wp).then_inc(weights_in, DMA)
                act.dma_start(w_p2[C:P, C:P], wp).then_inc(weights_in, DMA)
                act.dma_start(row_bv[:, :], row(bv)).then_inc(weights_in, DMA)
                act.dma_start(row_bp[:, :], row(bp)).then_inc(weights_in, DMA)
                act.dma_start(row_beta[:, :], row(beta)).then_inc(weights_in, DMA)
                copy_xT(0)
                act.wait_ge(biases_done, 3)
                split_hi(0)
                copy_xT(1)

            def image(b, u, prior, nxt, after):
                for i in range(T):
                    for h in range(2):
                        act.wait_ge(scores_made, 2 * T * b + 2 * i + h + 1)
                        if i >= E_RING:
                            act.wait_ge(pv_done, T * b + i - E_RING + 1)
                            act.wait_ge(sum_done, (T - 1) * b + max(i - E_RING, 1))
                        elif prior:
                            act.wait_ge(pv_done, T * b + i - E_RING + 1)
                            act.wait_ge(sum_done, (T - 1) * b + i - E_RING + 1)
                        nc.scalar.activation(probs[i % E_RING][:, h * HALF:(h + 1) * HALF],
                                             scores[:, h * HALF:(h + 1) * HALF], ACT.Exp,
                                             scale=SCALE).then_inc(exp_done, 1)
                    if i == 0:
                        if nxt:
                            split_hi(b + 1)
                        if prior:
                            copy_attn(b - 1)
                    if i == 2 and after:
                        copy_xT(b + 2)

            all_images(act, prologue, image)
            copy_attn(BATCH - 1)

        @block.vector
        def _(dve):
            def has_prior(b):
                return not isinstance(b, int) or b > 0

            def part_statistics(s):
                dve.wait_ge(xT_copied, s + 1)
                if has_prior(s):
                    dve.wait_ge(var_made, s)
                nc.vector.bn_stats(bn6[:, :], x_T[:, :]).then_inc(bn_done, 1)
                dve.wait_ge(bn_done, s + 1)
                nc.vector.tensor_scalar(var_terms[:, 2:4], part_moments, 2.0 / HALF, EPS, ALU.mult,
                                        ALU.add).then_inc(moments_done, 1)

            def mean_differences(s):
                dve.wait_ge(mean_made, s + 1)
                nc.vector.reduce_sum(group_mean_of[:, :], misc[:, 0:2], AX.X).then_inc(mean_done, 1)
                dve.wait_ge(mean_done, s + 1)
                nc.vector.tensor_scalar(mean_diff[:, :], part_means, group_mean_of[:, 0:1], None,
                                        ALU.subtract).then_inc(diff_done, 1)
                dve.wait_ge(diff_done, s + 1)
                nc.vector.tensor_tensor(var_terms[:, 0:2], mean_diff[:, :], mean_diff[:, :],
                                        ALU.mult).then_inc(diff2_done, 1)

            def variance(s):
                dve.wait_ge(var_made, s + 1)
                nc.vector.reduce_sum(var_eps[:, :], misc[:, 0:4], AX.X).then_inc(var_done, 1)

            def normalise(s, u):
                dve.wait_ge(rstd_done, s + 1)
                nc.vector.tensor_tensor(gain[:, :], rstd[:, :], gamma_col[:, :], ALU.mult).then_inc(gain_done, 1)
                dve.wait_ge(gain_done, s + 1)
                if has_prior(s):
                    dve.wait_ge(coef_made, s)
                nc.vector.tensor_scalar(diag[:, 0, :], identity[0:C, 0:C], gain[0:C, 0:1], None, ALU.mult)
                nc.vector.tensor_scalar(diag[:, 1, :], identity[0:C, 0:C], group_mean_of[0:C, 0:1], None,
                                        ALU.mult).then_inc(diag_done, 1)
                if has_prior(s):
                    dve.wait_ge(v_made, s)
                nc.vector.tensor_scalar(xn_T[:, :], x_T[:, :], group_mean_of[:, 0:1], gain[:, 0:1],
                                        ALU.subtract, ALU.mult).then_inc(xnT_done, 1)

            def residual_of(s, u):
                dve.wait_ge(coef_made, s + 1)
                nc.vector.tensor_tensor(pixels(centred[:, :]), pixels(x_in[u][:, :]), per_channel(misc[:, C:2 * C]),
                                        ALU.subtract).then_inc(centred_done, 1)
                dve.wait_ge(centred_done, s + 1)
                nc.vector.tensor_tensor(pixels(scaled[:, :]), pixels(centred[:, :]), per_channel(misc[:, 0:C]),
                                        ALU.mult).then_inc(scaled_done, 1)
                dve.wait_ge(scaled_done, s + 1)
                nc.vector.tensor_tensor(pixels(residual[:, bass.ds(s * (T * C), T * C)]), pixels(scaled[:, :]),
                                        per_channel(bias_out[:, :]), ALU.add).then_inc(residual_done, 1)

            def split_lo(p):
                for h in range(2):
                    half = slice(h * HALF, (h + 1) * HALF)
                    dve.wait_ge(hi_done, 2 * p + h + 1)
                    if h == 0 and has_prior(p):
                        dve.wait_ge(stacks_moved, MOVES * DMA * p)
                    nc.vector.scalar_tensor_tensor(lo[:, half], wide[0][:, half], bias_qk[:, 0:1],
                                                   hi[:, half].bitcast(fp32), ALU.add,
                                                   ALU.subtract).then_inc(lo_done, 1)

            def make_values(p, u):
                dve.wait_ge(v_made, p + 1)
                if not (isinstance(p, int) and p < 2):
                    dve.wait_ge(pv_done, T * (p - 1))
                nc.vector.tensor_tensor(pixels(values[u][:, :]), pixels(misc[:, :]), per_channel(bias_v[:, :]),
                                        ALU.add).then_inc(values_done, 1)

            def reduce_chunk(p, j):
                dve.wait_ge(wide_made, T * p + j + 1)
                if j == 0 and has_prior(p):
                    dve.wait_ge(maxT_made, p)
                nc.vector.reduce_max(chunk_max[:, j:j + 1], wide[j % 2][:, :], AX.X).then_inc(max_done, 1)

            def copy_maxT(p):
                dve.wait_ge(maxT_made, p + 1)
                if has_prior(p):
                    dve.wait_ge(max_placed, DMA * p)
                nc.vector.tensor_copy(max_T[:, :], misc[0:T, 0:P]).then_inc(maxT_done, 1)

            def finish(b, u):
                dve.wait_ge(sum_freed, b + 3)
                nc.vector.reciprocal(inv_den[:, :], wide[1][:, 0:T]).then_inc(inv_done, 1)
                dve.wait_ge(inv_done, b + 1)
                dve.wait_ge(y_made, b + 1)
                nc.vector.tensor_tensor(pixels(y_mul[:, :]), pixels(misc[:, :]),
                                        inv_den[:, :].unsqueeze(2).to_broadcast([P, T, C]),
                                        ALU.mult).then_inc(y_mul_done, 1)
                dve.wait_ge(y_mul_done, b + 1)
                dve.wait_ge(y_freed[u], (b - u) * (DMA // 2) + DMA)
                nc.vector.tensor_tensor(y_out[u][:, :], y_mul[:, :], residual[:, bass.ds(b * (T * C), T * C)],
                                        ALU.add).then_inc(y_done, 1)

            def prologue():
                nc.vector.memset(ones[:, :], 1.0).then_inc(fills_done, 1)
                nc.vector.memset(mean_diff[:, :], 0.0).then_inc(sum_freed, 2)
                for u in range(2):
                    nc.vector.memset(y_out[u][:, 0:1], 0.0).then_inc(y_freed[u], DMA)
                nc.vector.memset(minus_half[:, :], -0.5).then_inc(fills_done, 1)
                nc.vector.memset(w_v2[:, :], 0.0).then_inc(fills_done, 1)
                nc.vector.memset(w_p2[:, :], 0.0).then_inc(fills_done, 1)
                for u in range(2):
                    nc.vector.memset(queries_lo[u][C:P, :].bitcast(fp32), 0.0).then_inc(fills_done, 1)
                    nc.vector.memset(keys_guard[u][C:P, :].bitcast(fp32), 0.0).then_inc(fills_done, 1)
                dve.wait_ge(fills_done, 8)
                nc.vector.memset(keys_guard[0][C:C + 1, :].bitcast(fp32), -1.0).then_inc(fills_done, 1)
                nc.vector.memset(keys_guard[1][C:C + 1, :].bitcast(fp32), -1.0).then_inc(fills_done, 1)
                part_statistics(0)
                dve.wait_ge(weights_in, DMA * 18)
                nc.vector.tensor_copy(beta_wide[:, :], beta_col[:, 0:1].to_broadcast([C, P])).then_inc(beta_wide_done, 1)
                mean_differences(0)
                variance(0)
                normalise(0, 0)
                dve.wait_ge(biases_made, 1)
                nc.vector.tensor_tensor(bias_qk[:, :], attn[:, 0:1], bias_qk_in[:, :], ALU.add).then_inc(biases_done, 1)
                nc.vector.tensor_copy(bias_v[:, :], attn[:, C:2 * C]).then_inc(biases_done, 1)
                nc.vector.tensor_copy(bias_out[:, :], attn[:, 2 * C:3 * C]).then_inc(biases_done, 1)
                dve.wait_ge(biases_done, 3)
                residual_of(0, 0)
                split_lo(0)
                make_values(0, 0)
                part_statistics(1)
                mean_differences(1)
                variance(1)
                normalise(1, 1)
                residual_of(1, 1)
                for j in range(T):
                    reduce_chunk(0, j)
                copy_maxT(0)

            def image(b, u, prior, nxt, after):
                if nxt:
                    split_lo(b + 1)
                    make_values(b + 1, 1 - u)
                if prior:
                    finish(b - 1, 1 - u)
                if nxt:
                    reduce_chunk(b + 1, 0)
                    reduce_chunk(b + 1, 1)
                    if after:
                        part_statistics(b + 2)
                    reduce_chunk(b + 1, 2)
                    if after:
                        mean_differences(b + 2)
                    reduce_chunk(b + 1, 3)
                    reduce_chunk(b + 1, 4)
                    if after:
                        variance(b + 2)
                    reduce_chunk(b + 1, 5)
                    reduce_chunk(b + 1, 6)
                    reduce_chunk(b + 1, 7)
                    copy_maxT(b + 1)
                if after:
                    normalise(b + 2, u)
                    residual_of(b + 2, u)

            all_images(dve, prologue, image)
            finish(BATCH - 1, (BATCH - 1) % 2)

        @block.tensor
        def _(pe):
            def has_prior(b):
                return not isinstance(b, int) or b > 0

            def transpose_x(s, u, loads):
                pe.wait_ge(x_loaded[u], loads)
                for tt in range(PAIRS):
                    last = nc.tensor.transpose(misc[:, tt * P:(tt + 1) * P], x_in[u][:, tt * P:(tt + 1) * P],
                                               identity[:, :])
                last.then_inc(xT_made, 1)

            def group_means(s):
                pe.wait_ge(bn_done, s + 1)
                nc.tensor.matmul(misc[:, 0:2], group_mean[:, :], part_means, start=True,
                                 stop=True).then_inc(mean_made, 1)

            def group_variances(s):
                pe.wait_ge(moments_done, s + 1)
                pe.wait_ge(diff2_done, s + 1)
                nc.tensor.matmul(misc[:, 0:4], group_mean[:, :], var_terms[:, :], start=True,
                                 stop=True).then_inc(var_made, 1)

            def coefficients(s):
                pe.wait_ge(diag_done, s + 1)
                nc.tensor.matmul(misc[:, 0:2 * C], ones[0:C, :], diag[:, :, :].rearrange("p a c -> p (a c)"),
                                 start=True, stop=True).then_inc(coef_made, 1)

            def project_qk(p):
                pe.wait_ge(xnT_done, p + 1)
                for tp in range(2):
                    nc.tensor.matmul(wide[0][:, tp * HALF:(tp + 1) * HALF], w_qk[tp * C:(tp + 1) * C, :],
                                     xn_T[tp * C:(tp + 1) * C, :], start=True, stop=True).then_inc(qk_made, 1)

            def project_v(p):
                pe.wait_ge(scaled_done, p + 1)
                if has_prior(p):
                    pe.wait_ge(maxT_done, p)
                for tt in range(PAIRS):
                    last = nc.tensor.matmul(misc[:, tt * P:(tt + 1) * P], xn_T[:, tt * P:(tt + 1) * P], w_v2[:, :],
                                            start=True, stop=True)
                last.then_inc(v_made, 1)

            def max_chunk(p, u, j):
                if j == 0:
                    pe.wait_ge(stacks_moved, MOVES * DMA * (p + 1))
                    pe.wait_ge(lo_done, 2 * p + 2)
                elif j == 1:
                    if has_prior(p - 1 if isinstance(p, int) else p):
                        pe.wait_ge(inv_done, p - 1)
                else:
                    pe.wait_ge(max_done, T * p + j - 1)
                for h in range(2):
                    last = nc.tensor.matmul(wide[j % 2][:, h * HALF:(h + 1) * HALF],
                                            queries_hi[u][:, j * P:(j + 1) * P],
                                            keys_hilo[u][:, h * HALF:(h + 1) * HALF], start=True, stop=True)
                last.then_inc(wide_made, 1)

            def transpose_max(p):
                pe.wait_ge(max_done, T * p + T)
                nc.tensor.matmul(misc[0:T, 0:P], chunk_max[:, :], identity[:, :], start=True,
                                 stop=True).then_inc(maxT_made, 1)

            def score_tile(b, u, i):
                if i == 0:
                    pe.wait_ge(max_placed, DMA * (b + 1))
                for h in range(2):
                    half = slice(h * HALF, (h + 1) * HALF)
                    if i > 0:
                        pe.wait_ge(exp_done, 2 * T * b + 2 * i - 1 + h)
                    elif has_prior(b):
                        pe.wait_ge(exp_done, 2 * T * b - 1 + h)
                    nc.tensor.matmul(scores[:, half], keys_hilo[u][:, i * P:(i + 1) * P], queries_hi[u][:, half],
                                     start=True, stop=False)
                    nc.tensor.matmul(scores[:, half], keys_guard[u][:, i * P:(i + 1) * P], queries_lo[u][:, half],
                                     start=False, stop=True).then_inc(scores_made, 1)

            def weigh_values(b, u, i):
                tp, tt = divmod(i, PAIRS)
                v = values[u][:, (2 * tt + tp) * C:(2 * tt + tp + 1) * C]
                pe.wait_ge(exp_done, 2 * T * b + 2 * i + 2)
                if i == 0:
                    pe.wait_ge(values_done, b + 1)
                    if has_prior(b):
                        pe.wait_ge(attnT_done, b)
                nc.tensor.matmul(attn[0:C, :], v, probs[i % E_RING][:, 0:HALF], start=(i == 0), stop=(i == T - 1),
                                 skip_group_check=True)
                nc.tensor.matmul(attn[C:P, :], v, probs[i % E_RING][:, HALF:PIXELS], start=(i == 0),
                                 stop=(i == T - 1), skip_group_check=True).then_inc(pv_done, 1)

            def project_out(b):
                pe.wait_ge(attnT_done, b + 1)
                for tt in range(PAIRS):
                    last = nc.tensor.matmul(misc[:, tt * P:(tt + 1) * P], attn_T[:, tt * P:(tt + 1) * P], w_p2[:, :],
                                            start=True, stop=True)
                last.then_inc(y_made, 1)

            def denominators(b, u):
                pe.wait_ge(sum_done, (T - 1) * (b + 1))
                for j in range(T):
                    tp, tt = divmod(j, PAIRS)
                    last = nc.tensor.matmul(wide[1][:, 2 * tt + tp:2 * tt + tp + 1],
                                            prob_sum[u][:, j * P:(j + 1) * P], ones[:, 0:1], start=True, stop=True)
                last.then_inc(sum_freed, 1)

            def prologue():
                pe.wait_ge(weights_in, DMA * 18)
                pe.wait_ge(fills_done, FILLS)
                transpose_x(0, 0, DMA)
                pe.wait_ge(beta_wide_done, 1)
                nc.tensor.matmul(attn[:, 0:1], w_qk[0:C, :], beta_col[:, :], start=True, stop=True)
                nc.tensor.matmul(attn[:, C:2 * C], beta_wide[:, :], w_v2[0:C, 0:C], start=True, stop=False)
                nc.tensor.matmul(attn[:, C:2 * C], ones[0:1, :], row_bv[:, :], start=False, stop=True)
                nc.tensor.matmul(attn[:, 2 * C:3 * C], ones[0:1, :], row_beta[:, :], start=True, stop=False)
                nc.tensor.matmul(attn[:, 2 * C:3 * C], ones[0:1, :], row_bp[:, :], start=False,
                                 stop=True).then_inc(biases_made, 1)
                group_means(0)
                group_variances(0)
                coefficients(0)
                project_qk(0)
                project_v(0)
                pe.wait_ge(values_done, 1)
                transpose_x(1, 1, DMA)
                group_means(1)
                group_variances(1)
                coefficients(1)
                for j in range(T):
                    max_chunk(0, 0, j)
                pe.wait_ge(scaled_done, 2)
                transpose_max(0)

            def image(b, u, prior, nxt, after):
                v = 1 - u
                score_tile(b, u, 0)
                if nxt:
                    project_qk(b + 1)
                if prior:
                    weigh_values(b - 1, v, T - 1)
                if nxt:
                    project_v(b + 1)
                score_tile(b, u, 1)
                if prior:
                    if nxt:
                        pe.wait_ge(values_done, b + 2)
                    project_out(b - 1)
                    if nxt:
                        pe.wait_ge(lo_done, 2 * (b + 1) + 2)
                    denominators(b - 1, v)
                weigh_values(b, u, 0)
                for i in range(2, T):
                    score_tile(b, u, i)
                    if nxt and i < 6:
                        max_chunk(b + 1, v, 2 * (i - 2))
                    if after and i == 2:
                        if prior:
                            pe.wait_ge(y_mul_done, b)
                        else:
                            pe.wait_ge(values_done, b + 2)
                        transpose_x(b + 2, u, (b - u) * (DMA // 2) + 2 * DMA)
                    if after and i == 3:
                        group_means(b + 2)
                    if after and i == 4:
                        group_variances(b + 2)
                    if nxt and i == 6:
                        if after:
                            pe.wait_ge(var_done, b + 3)
                        transpose_max(b + 1)
                    if after and i == 7:
                        pe.wait_ge(maxT_done, b + 2)
                        coefficients(b + 2)
                    weigh_values(b, u, i - 1)
                    if nxt and i < 6:
                        max_chunk(b + 1, v, 2 * (i - 2) + 1)

            all_images(pe, prologue, image)
            weigh_values(BATCH - 1, (BATCH - 1) % 2, T - 1)
            pe.wait_ge(inv_done, BATCH - 1)
            denominators(BATCH - 1, (BATCH - 1) % 2)
            pe.wait_ge(y_mul_done, BATCH - 1)
            project_out(BATCH - 1)


_INS = ["x", "L0_conv_gamma", "L0_conv_beta", "L0_conv_wq", "L0_conv_bq", "L0_conv_wk", "L0_conv_bk",
        "L0_conv_wv", "L0_conv_bv", "L0_conv_wp", "L0_conv_bp"]


def kernel(**inputs):
    import numpy as _np
    import concourse.bacc as _bacc
    from concourse import mybir as _mybir
    from concourse.bass_utils import run_bass_kernel_spmd as _run

    nc = _bacc.Bacc("TRN2", target_bir_lowering=False, num_devices=1)
    arrays, args = {}, []
    for name in _INS:
        a = _np.ascontiguousarray(inputs[name])
        arrays[f"in_{name}_dram"] = a
        args.append(nc.dram_tensor(f"in_{name}_dram", a.shape, _mybir.dt.from_np(a.dtype), kind="ExternalInput").ap())
    channels = inputs["x"].shape[-1]
    width = channels // 8
    group = (_np.arange(2 * channels) % channels) // width
    constants = {"identity": _np.eye(2 * channels, dtype=_np.float32),
                 "group_mean": (group[:, None] == group[None, :]).astype(_np.float32) / _np.float32(4 * width)}
    for name, a in constants.items():
        arrays[f"const_{name}_dram"] = a
        args.append(nc.dram_tensor(f"const_{name}_dram", a.shape, _mybir.dt.float32, kind="ExternalInput").ap())
    shape = inputs["x"].shape
    out = nc.dram_tensor("out_0_dram", shape, _mybir.dt.float32, kind="ExternalOutput").ap()
    attention_block(nc, *args, out)
    r = _run(nc, [arrays], core_ids=[0])
    return r.results[0]["out_0_dram"]
```

```python
import numpy as np
import concourse.bass as bass
from concourse import mybir
from contextlib import ExitStack



def attention_block(nc, x, beta, bv, bp, packed_in, out):
    fp32 = mybir.dt.float32
    fp32r = mybir.dt.float32r
    ALU = mybir.AluOpType
    ACT = mybir.ActivationFunctionType
    AX = mybir.AxisListType

    BATCH, HEIGHT, WIDTH, C = x.shape
    PIXELS = HEIGHT * WIDTH
    P = 128
    T = PIXELS // P
    HALF = PIXELS // 2
    PAIRS = T // 2
    GROUPS = 4
    ROWS = P // GROUPS
    SCALE = float(C) ** -0.5
    EPS = 1e-5
    E_RING = 4
    RSTD_AT = 4
    DMA = 16
    MAX_MOVES = 4
    SCORE_MOVES = 2

    x_nat = x.rearrange("b h w c -> b (h w) c").rearrange("b (p t) c -> b p (t c)", p=P)
    out_nat = out.rearrange("b h w c -> b (h w) c").rearrange("b (p t) c -> b p (t c)", p=P)

    def in_all_partitions(v):
        return v.rearrange("(o c) -> o c", o=1).to_broadcast([P, C])

    ctx = ExitStack()
    with ctx:
        def sb(name, shape, dt=fp32):
            return ctx.enter_context(nc.sbuf_tensor(name, shape, dt))

        def ps(name, shape):
            return ctx.enter_context(nc.psum_tensor(name, shape, fp32))

        def sem(name):
            return ctx.enter_context(nc.semaphore(name))

        packed = sb("packed", [P, packed_in.shape[1]])
        identity = packed[:, 0:P]
        group_mean = packed[:, P:2 * P]
        w_qk = packed[:, 2 * P:3 * P]
        w_vp = packed[:, 3 * P:4 * P]
        gamma_col = packed[:, 4 * P:4 * P + 1]
        beta_col = packed[0:C, 4 * P + 1:4 * P + 2]
        bias_qk_in = packed[:, 4 * P + 2:4 * P + 3]
        w_v2 = sb("w_v2", [P, P])
        w_p2 = sb("w_p2", [P, P])
        ones = sb("ones", [P, P])
        beta_wide = sb("beta_wide", [C, P])
        bias_qk = sb("bias_qk", [P, 1])
        bv_all = sb("bv_all", [P, C])
        bp_all = sb("bp_all", [P, C])
        beta_all = sb("beta_all", [P, C])
        bias_v = sb("bias_v", [P, C])
        bias_out = sb("bias_out", [P, C])
        x_in = [sb(f"x_in{u}", [P, T * C]) for u in range(2)]
        x_T = sb("x_T", [P, HALF])
        xn_T = sb("xn_T", [P, HALF])
        bn6 = sb("bn6", [P, 6])
        part_means = bn6[:, 1:6:3]
        part_moments = bn6[:, 2:6:3]
        group_mean_of = sb("group_mean_of", [P, 1])
        mean_diff = sb("mean_diff", [P, 2])
        var_terms = sb("var_terms", [P, 4])
        var_eps = sb("var_eps", [P, 1])
        minus_half = sb("minus_half", [P, 1])
        rstd = sb("rstd", [P, 1])
        gain = sb("gain", [P, 1])
        diag = sb("diag", [C, 2, C])
        residual = sb("residual", [P, BATCH * T * C])
        centred = sb("centred", [P, T * C])
        scaled = sb("scaled", [P, T * C])
        hi = sb("hi", [P, PIXELS], fp32r)
        lo = sb("lo", [P, PIXELS], fp32r)
        queries_hi = [sb(f"queries_hi{u}", [P, PIXELS], fp32r) for u in range(2)]
        queries_lo = [sb(f"queries_lo{u}", [C + 1, PIXELS], fp32r) for u in range(2)]
        keys_hilo = [sb(f"keys_hilo{u}", [P, PIXELS], fp32r) for u in range(2)]
        keys_guard = [sb(f"keys_guard{u}", [C + 1, PIXELS], fp32r) for u in range(2)]
        values = [sb(f"values{u}", [P, T * C]) for u in range(2)]
        chunk_max = sb("chunk_max", [P, T])
        max_T = sb("max_T", [T, P], fp32r)
        probs = [sb(f"probs{k}", [P, PIXELS]) for k in range(E_RING)]
        prob_sum = [sb(f"prob_sum{u}", [P, PIXELS]) for u in range(2)]
        attn_T = sb("attn_T", [P, HALF])
        den_rows = sb("den_rows", [P, PIXELS // GROUPS])
        inv_den = sb("inv_den", [P, T])
        y_mul = sb("y_mul", [P, T * C])
        y_out = [sb(f"y_out{u}", [P, T * C]) for u in range(2)]

        scores = ps("scores", [P, PIXELS])
        wide = [ps(f"wide{k}", [P, PIXELS]) for k in range(2)]
        attn = ps("attn", [P, HALF])
        misc = ps("misc", [P, HALF])

        packed_loaded = sem("packed_loaded")
        rows_loaded = sem("rows_loaded")
        x_loaded = [sem(f"x_loaded{u}") for u in range(2)]
        max_stacks_moved = sem("max_stacks_moved")
        score_stacks_moved = sem("score_stacks_moved")
        max_placed = sem("max_placed")
        y_freed = [sem(f"y_freed{u}") for u in range(2)]
        ones_done = sem("ones_done")
        guard_done = sem("guard_done")
        half_done = sem("half_done")
        zeros_done = sem("zeros_done")
        blocks_done = sem("blocks_done")
        beta_wide_done = sem("beta_wide_done")
        biases_made = sem("biases_made")
        biases_done = sem("biases_done")
        xT_made = sem("xT_made")
        xT_copied = sem("xT_copied")
        bn_done = sem("bn_done")
        moments_done = sem("moments_done")
        mean_made = sem("mean_made")
        mean_done = sem("mean_done")
        diff_done = sem("diff_done")
        diff2_done = sem("diff2_done")
        var_made = sem("var_made")
        var_done = sem("var_done")
        rstd_done = sem("rstd_done")
        gain_done = sem("gain_done")
        xnT_done = sem("xnT_done")
        diag_done = sem("diag_done")
        coef_made = sem("coef_made")
        centred_done = sem("centred_done")
        scaled_done = sem("scaled_done")
        residual_done = sem("residual_done")
        qk_made = sem("qk_made")
        hi_done = sem("hi_done")
        lo_done = sem("lo_done")
        v_made = sem("v_made")
        values_done = sem("values_done")
        wide_made = sem("wide_made")
        max_done = sem("max_done")
        maxT_made = sem("maxT_made")
        maxT_done = sem("maxT_done")
        scores_made = sem("scores_made")
        exp_done = sem("exp_done")
        pv_done = sem("pv_done")
        sum_done = sem("sum_done")
        last_sum_done = sem("last_sum_done")
        attnT_done = sem("attnT_done")
        y_made = sem("y_made")
        sum_freed = sem("sum_freed")
        den_copied = sem("den_copied")
        den_turned = sem("den_turned")
        inv_done = sem("inv_done")
        y_mul_done = sem("y_mul_done")
        y_done = sem("y_done")

        def per_channel(ap):
            return ap.unsqueeze(1).to_broadcast([P, T, C])

        def pixels(ap):
            return ap.rearrange("p (t c) -> p t c", t=T)

        FIRST, LOOP_FROM, LOOP_TO = 0, 1, BATCH - 3

        def all_images(eng, prologue, image):
            prologue()
            image(FIRST, FIRST % 2, prior=False, nxt=True, after=True)
            with eng.Fori(LOOP_FROM, LOOP_TO, 2) as b:
                image(b, LOOP_FROM % 2, prior=True, nxt=True, after=True)
                image(b + 1, (LOOP_FROM + 1) % 2, prior=True, nxt=True, after=True)
            image(BATCH - 3, (BATCH - 3) % 2, prior=True, nxt=True, after=True)
            image(BATCH - 2, (BATCH - 2) % 2, prior=True, nxt=True, after=False)
            image(BATCH - 1, (BATCH - 1) % 2, prior=True, nxt=False, after=False)

        block = ctx.enter_context(nc.Block())

        @block.sync
        def _(sp):
            def load_x(b, u):
                sp.dma_start(x_in[u][:, :], x_nat[bass.ds(b, 1)].rearrange("o p f -> (o p) f")).then_inc(x_loaded[u], DMA)

            def stack(p, u):
                def move(to, of, moved):
                    sp.dma_start(to.bitcast(fp32), of.bitcast(fp32)).then_inc(moved, DMA)

                sp.wait_ge(hi_done, 2 * p + 2)
                move(queries_hi[u][0:C, :], hi[0:C, :], max_stacks_moved)
                move(queries_hi[u][C:P, :], hi[0:C, :], max_stacks_moved)
                move(keys_hilo[u][0:C, :], hi[C:P, :], max_stacks_moved)
                sp.wait_ge(lo_done, 2 * p + 2)
                move(keys_hilo[u][C:P, :], lo[C:P, :], max_stacks_moved)
                move(keys_guard[u][0:C, :], hi[C:P, :], score_stacks_moved)
                move(queries_lo[u][0:C, :], lo[0:C, :], score_stacks_moved)

            def place_max(p, u):
                sp.wait_ge(maxT_done, p + 1)
                sp.dma_start(queries_lo[u][C:C + 1, :].bitcast(fp32).rearrange("o (t q) -> o t q", t=T),
                             max_T[:, :].bitcast(fp32)).then_inc(max_placed, DMA)

            def store(b, u):
                sp.wait_ge(y_done, b + 1)
                sp.dma_start(out_nat[bass.ds(b, 1)].rearrange("o p f -> (o p) f"), y_out[u][:, :]).then_inc(y_freed[u], DMA)

            def prologue():
                load_x(0, 0)
                sp.dma_start(packed[:, :], packed_in).then_inc(packed_loaded, DMA)
                load_x(1, 1)
                sp.dma_start(bv_all[:, :], in_all_partitions(bv)).then_inc(rows_loaded, DMA)
                sp.dma_start(bp_all[:, :], in_all_partitions(bp)).then_inc(rows_loaded, DMA)
                sp.dma_start(beta_all[:, :], in_all_partitions(beta)).then_inc(rows_loaded, DMA)
                stack(0, 0)
                place_max(0, 0)

            def image(b, u, prior, nxt, after):
                if after:
                    sp.wait_ge(centred_done, b + 1)
                    load_x(b + 2, u)
                if nxt:
                    stack(b + 1, 1 - u)
                if nxt:
                    place_max(b + 1, 1 - u)
                if prior:
                    store(b - 1, 1 - u)

            all_images(sp, prologue, image)
            store(BATCH - 1, (BATCH - 1) % 2)
            for u in range(2):
                sp.wait_ge(y_freed[u], DMA * (BATCH // 2 + 1))

        @block.gpsimd
        def _(pool):
            def rstd_of(s):
                pool.wait_ge(var_done, s + 1)
                if not isinstance(s, int) or s > 0:
                    pool.wait_ge(gain_done, s)
                nc.gpsimd.tensor_tensor(rstd[:, :], var_eps[:, :], minus_half[:, :], ALU.pow).then_inc(rstd_done, 1)

            def prologue():
                nc.gpsimd.memset(minus_half[:, :], -0.5).then_inc(half_done, 1)
                pool.wait_ge(half_done, 1)
                for u in range(2):
                    nc.gpsimd.memset(keys_guard[u][C:C + 1, :].bitcast(fp32), -1.0).then_inc(guard_done, 1)
                    pool.wait_ge(guard_done, u + 1)
                rstd_of(0)
                rstd_of(1)

            def image(b, u, prior, nxt, after):
                if not nxt:
                    return
                for i in range(1, T):
                    pool.wait_ge(exp_done, 2 * T * b + 2 * i + 2)
                    if i == 1:
                        pool.wait_ge(sum_freed, b + 1)
                        first = probs[0]
                    else:
                        pool.wait_ge(sum_done, (T - 1) * b + i - 1)
                        first = prob_sum[u]
                    nc.gpsimd.tensor_tensor(prob_sum[u][:, :], first[:, :], probs[i % E_RING][:, :],
                                            ALU.add).then_inc(sum_done, 1)
                    if i == RSTD_AT and after:
                        rstd_of(b + 2)

            all_images(pool, prologue, image)

        @block.scalar
        def _(act):
            def copy_xT(s):
                act.wait_ge(xT_made, s + 1)
                if not isinstance(s, int) or s > 0:
                    act.wait_ge(xnT_done, s)
                nc.scalar.copy(x_T[:, :], misc[:, :]).then_inc(xT_copied, 1)

            def split_hi(p):
                for h in range(2):
                    act.wait_ge(qk_made, 2 * p + h + 1)
                    if h == 0 and (not isinstance(p, int) or p > 0):
                        act.wait_ge(max_stacks_moved, MAX_MOVES * DMA * p)
                        act.wait_ge(score_stacks_moved, SCORE_MOVES * DMA * p)
                    nc.scalar.activation(hi[:, h * HALF:(h + 1) * HALF], wide[0][:, h * HALF:(h + 1) * HALF],
                                         ACT.Identity, bias=bias_qk[:, 0:1]).then_inc(hi_done, 1)

            def copy_attn(b):
                act.wait_ge(pv_done, T * b + T)
                if not isinstance(b, int) or b > 0:
                    act.wait_ge(y_made, b)
                nc.scalar.copy(attn_T[:, :], attn[:, :]).then_inc(attnT_done, 1)

            def prologue():
                copy_xT(0)
                act.wait_ge(biases_done, 3)
                split_hi(0)
                copy_xT(1)

            def image(b, u, prior, nxt, after):
                if nxt:
                    split_hi(b + 1)
                for i in range(T):
                    for h in range(2):
                        act.wait_ge(scores_made, 2 * T * b + 2 * i + h + 1)
                        if i >= E_RING:
                            act.wait_ge(pv_done, T * b + i - E_RING + 1)
                            summed = max(i - E_RING, 1)
                            if nxt:
                                act.wait_ge(sum_done, (T - 1) * b + summed)
                            else:
                                act.wait_ge(last_sum_done, summed)
                        elif prior:
                            act.wait_ge(pv_done, T * b + i - E_RING + 1)
                            act.wait_ge(sum_done, (T - 1) * b + i - E_RING + 1)
                        nc.scalar.activation(probs[i % E_RING][:, h * HALF:(h + 1) * HALF],
                                             scores[:, h * HALF:(h + 1) * HALF], ACT.Exp,
                                             scale=SCALE).then_inc(exp_done, 1)
                    if i == 0 and prior:
                        copy_attn(b - 1)
                    if i == 1 and after:
                        copy_xT(b + 2)

            all_images(act, prologue, image)
            copy_attn(BATCH - 1)

        @block.vector
        def _(dve):
            def has_prior(b):
                return not isinstance(b, int) or b > 0

            def part_statistics(s):
                dve.wait_ge(xT_copied, s + 1)
                if has_prior(s):
                    dve.wait_ge(var_made, s)
                nc.vector.bn_stats(bn6[:, :], x_T[:, :]).then_inc(bn_done, 1)
                dve.wait_ge(bn_done, s + 1)
                nc.vector.tensor_scalar(var_terms[:, 2:4], part_moments, 2.0 / HALF, EPS, ALU.mult,
                                        ALU.add).then_inc(moments_done, 1)

            def mean_differences(s):
                dve.wait_ge(mean_made, s + 1)
                nc.vector.reduce_sum(group_mean_of[:, :], misc[:, 0:2], AX.X).then_inc(mean_done, 1)
                dve.wait_ge(mean_done, s + 1)
                nc.vector.tensor_scalar(mean_diff[:, :], part_means, group_mean_of[:, 0:1], None,
                                        ALU.subtract).then_inc(diff_done, 1)
                dve.wait_ge(diff_done, s + 1)
                nc.vector.tensor_tensor(var_terms[:, 0:2], mean_diff[:, :], mean_diff[:, :],
                                        ALU.mult).then_inc(diff2_done, 1)

            def variance(s):
                dve.wait_ge(var_made, s + 1)
                nc.vector.reduce_sum(var_eps[:, :], misc[:, 0:4], AX.X).then_inc(var_done, 1)

            def normalise(s, u):
                dve.wait_ge(rstd_done, s + 1)
                nc.vector.tensor_tensor(gain[:, :], rstd[:, :], gamma_col[:, :], ALU.mult).then_inc(gain_done, 1)
                dve.wait_ge(gain_done, s + 1)
                if has_prior(s):
                    dve.wait_ge(coef_made, s)
                nc.vector.tensor_scalar(diag[:, 0, :], identity[0:C, 0:C], gain[0:C, 0:1], None, ALU.mult)
                nc.vector.tensor_scalar(diag[:, 1, :], identity[0:C, 0:C], group_mean_of[0:C, 0:1], None,
                                        ALU.mult).then_inc(diag_done, 1)
                if has_prior(s):
                    dve.wait_ge(v_made, s)
                nc.vector.tensor_scalar(xn_T[:, :], x_T[:, :], group_mean_of[:, 0:1], gain[:, 0:1],
                                        ALU.subtract, ALU.mult).then_inc(xnT_done, 1)

            def residual_of(s, u):
                dve.wait_ge(coef_made, s + 1)
                nc.vector.tensor_tensor(pixels(centred[:, :]), pixels(x_in[u][:, :]), per_channel(misc[:, C:2 * C]),
                                        ALU.subtract).then_inc(centred_done, 1)
                dve.wait_ge(centred_done, s + 1)
                nc.vector.tensor_tensor(pixels(scaled[:, :]), pixels(centred[:, :]), per_channel(misc[:, 0:C]),
                                        ALU.mult).then_inc(scaled_done, 1)
                dve.wait_ge(scaled_done, s + 1)
                nc.vector.tensor_tensor(pixels(residual[:, bass.ds(s * (T * C), T * C)]), pixels(scaled[:, :]),
                                        per_channel(bias_out[:, :]), ALU.add).then_inc(residual_done, 1)

            def split_lo(p):
                for h in range(2):
                    half = slice(h * HALF, (h + 1) * HALF)
                    dve.wait_ge(hi_done, 2 * p + h + 1)
                    if h == 0 and has_prior(p):
                        dve.wait_ge(max_stacks_moved, MAX_MOVES * DMA * p)
                        dve.wait_ge(score_stacks_moved, SCORE_MOVES * DMA * p)
                    nc.vector.scalar_tensor_tensor(lo[:, half], wide[0][:, half], bias_qk[:, 0:1],
                                                   hi[:, half].bitcast(fp32), ALU.add,
                                                   ALU.subtract).then_inc(lo_done, 1)

            def make_values(p, u):
                dve.wait_ge(v_made, p + 1)
                if not (isinstance(p, int) and p < 2):
                    dve.wait_ge(pv_done, T * (p - 1))
                nc.vector.tensor_tensor(pixels(values[u][:, :]), pixels(misc[:, :]), per_channel(bias_v[:, :]),
                                        ALU.add).then_inc(values_done, 1)

            def reduce_chunk(p, j):
                dve.wait_ge(wide_made, T * p + j + 1)
                if j == 0 and has_prior(p):
                    dve.wait_ge(maxT_made, p)
                nc.vector.reduce_max(chunk_max[:, j:j + 1], wide[j % 2][:, :], AX.X).then_inc(max_done, 1)

            def copy_maxT(p):
                dve.wait_ge(maxT_made, p + 1)
                if has_prior(p):
                    dve.wait_ge(max_placed, DMA * p)
                nc.vector.tensor_copy(max_T[:, :], misc[0:T, 0:P]).then_inc(maxT_done, 1)

            def copy_den(b):
                dve.wait_ge(sum_freed, b + 3)
                nc.vector.tensor_copy(den_rows[:, :], misc[:, 0:PIXELS // GROUPS]).then_inc(den_copied, 1)

            def invert(b):
                dve.wait_ge(den_turned, b + 1)
                turned = misc[:, 0:2 * P:ROWS].rearrange("p (k a c) -> p k a c", k=2, a=2)
                nc.vector.reciprocal(inv_den[:, :].rearrange("p (c k a) -> p k a c", c=2, k=2), turned).then_inc(inv_done, 1)

            def finish(b, u):
                dve.wait_ge(inv_done, b + 1)
                dve.wait_ge(y_made, b + 1)
                nc.vector.tensor_tensor(pixels(y_mul[:, :]), pixels(wide[1][:, 0:HALF]),
                                        inv_den[:, :].unsqueeze(2).to_broadcast([P, T, C]),
                                        ALU.mult).then_inc(y_mul_done, 1)
                dve.wait_ge(y_mul_done, b + 1)
                dve.wait_ge(y_freed[u], (b - u) * (DMA // 2) + DMA)
                nc.vector.tensor_tensor(y_out[u][:, :], y_mul[:, :], residual[:, bass.ds(b * (T * C), T * C)],
                                        ALU.add).then_inc(y_done, 1)

            def sum_probs(b, u, i):
                dve.wait_ge(exp_done, 2 * T * b + 2 * i + 2)
                if i == 1:
                    dve.wait_ge(sum_freed, b + 1)
                    first = probs[0]
                else:
                    dve.wait_ge(last_sum_done, i - 1)
                    first = prob_sum[u]
                nc.vector.tensor_tensor(prob_sum[u][:, :], first[:, :], probs[i % E_RING][:, :],
                                        ALU.add).then_inc(last_sum_done, 1)

            def prologue():
                nc.vector.memset(ones[:, :], 1.0).then_inc(ones_done, 1)
                nc.vector.memset(w_v2[:, :], 0.0).then_inc(zeros_done, 1)
                nc.vector.memset(w_p2[:, :], 0.0).then_inc(zeros_done, 1)
                nc.vector.memset(mean_diff[:, :], 0.0).then_inc(sum_freed, 2)
                for u in range(2):
                    nc.vector.memset(y_out[u][:, 0:1], 0.0).then_inc(y_freed[u], DMA)
                dve.wait_ge(packed_loaded, DMA)
                dve.wait_ge(zeros_done, 2)
                for rows in (slice(0, C), slice(C, P)):
                    nc.vector.tensor_copy(w_v2[rows, rows], w_vp[rows, 0:C]).then_inc(blocks_done, 1)
                    nc.vector.tensor_copy(w_p2[rows, rows], w_vp[rows, C:P]).then_inc(blocks_done, 1)
                nc.vector.tensor_copy(beta_wide[:, :], beta_col.to_broadcast([C, P])).then_inc(beta_wide_done, 1)
                part_statistics(0)
                mean_differences(0)
                variance(0)
                normalise(0, 0)
                dve.wait_ge(biases_made, 1)
                nc.vector.tensor_tensor(bias_qk[:, :], attn[:, 0:1], bias_qk_in, ALU.add).then_inc(biases_done, 1)
                dve.wait_ge(rows_loaded, 3 * DMA)
                nc.vector.tensor_tensor(bias_v[:, :], attn[:, C:2 * C], bv_all[:, :], ALU.add).then_inc(biases_done, 1)
                nc.vector.tensor_tensor(bias_out[:, :], beta_all[:, :], bp_all[:, :], ALU.add).then_inc(biases_done, 1)
                dve.wait_ge(biases_done, 3)
                split_lo(0)
                make_values(0, 0)
                residual_of(0, 0)
                reduce_chunk(0, 0)
                reduce_chunk(0, 1)
                part_statistics(1)
                reduce_chunk(0, 2)
                reduce_chunk(0, 3)
                mean_differences(1)
                reduce_chunk(0, 4)
                reduce_chunk(0, 5)
                variance(1)
                reduce_chunk(0, 6)
                reduce_chunk(0, 7)
                copy_maxT(0)
                normalise(1, 1)
                residual_of(1, 1)

            def image(b, u, prior, nxt, after):
                p, s, v = b + 1, b + 2, 1 - u
                if not nxt:
                    for i in range(1, T):
                        sum_probs(b, u, i)
                        if i == 1:
                            copy_den(b - 1)
                        if i == 2:
                            invert(b - 1)
                        if i == 4:
                            finish(b - 1, v)
                    return
                split_lo(p)
                make_values(p, v)
                if after:
                    part_statistics(s)
                reduce_chunk(p, 0)
                if after:
                    mean_differences(s)
                reduce_chunk(p, 1)
                reduce_chunk(p, 2)
                if after:
                    variance(s)
                reduce_chunk(p, 3)
                if prior:
                    copy_den(b - 1)
                reduce_chunk(p, 4)
                if prior:
                    invert(b - 1)
                reduce_chunk(p, 5)
                reduce_chunk(p, 6)
                reduce_chunk(p, 7)
                copy_maxT(p)
                if after:
                    normalise(s, u)
                if prior:
                    finish(b - 1, v)
                if after:
                    residual_of(s, u)

            all_images(dve, prologue, image)
            copy_den(BATCH - 1)
            invert(BATCH - 1)
            finish(BATCH - 1, (BATCH - 1) % 2)

        @block.tensor
        def _(pe):
            def has_prior(b):
                return not isinstance(b, int) or b > 0

            def transpose_x(s, u, loads):
                pe.wait_ge(x_loaded[u], loads)
                for tt in range(PAIRS):
                    last = nc.tensor.transpose(misc[:, tt * P:(tt + 1) * P], x_in[u][:, tt * P:(tt + 1) * P],
                                               identity)
                last.then_inc(xT_made, 1)

            def group_means(s):
                pe.wait_ge(bn_done, s + 1)
                nc.tensor.matmul(misc[:, 0:2], group_mean, part_means, start=True,
                                 stop=True).then_inc(mean_made, 1)

            def group_variances(s):
                pe.wait_ge(moments_done, s + 1)
                pe.wait_ge(diff2_done, s + 1)
                nc.tensor.matmul(misc[:, 0:4], group_mean, var_terms[:, :], start=True,
                                 stop=True).then_inc(var_made, 1)

            def coefficients(s):
                pe.wait_ge(diag_done, s + 1)
                nc.tensor.matmul(misc[:, 0:2 * C], ones[0:C, :], diag[:, :, :].rearrange("p a c -> p (a c)"),
                                 start=True, stop=True).then_inc(coef_made, 1)

            def project_qk(p):
                pe.wait_ge(xnT_done, p + 1)
                for tp in range(2):
                    nc.tensor.matmul(wide[0][:, tp * HALF:(tp + 1) * HALF], w_qk[tp * C:(tp + 1) * C, :],
                                     xn_T[tp * C:(tp + 1) * C, :], start=True, stop=True).then_inc(qk_made, 1)

            def project_v(p):
                if has_prior(p):
                    pe.wait_ge(scaled_done, p + 1)
                for tt in range(PAIRS):
                    last = nc.tensor.matmul(misc[:, tt * P:(tt + 1) * P], xn_T[:, tt * P:(tt + 1) * P], w_v2[:, :],
                                            start=True, stop=True)
                last.then_inc(v_made, 1)

            def max_chunk(p, u, j):
                if j == 0:
                    pe.wait_ge(max_stacks_moved, MAX_MOVES * DMA * (p + 1))
                    pe.wait_ge(lo_done, 2 * p + 2)
                elif j == 1:
                    if has_prior(p - 1 if isinstance(p, int) else p) and not (isinstance(p, int) and p == 2):
                        pe.wait_ge(y_mul_done, p - 2)
                else:
                    pe.wait_ge(max_done, T * p + j - 1)
                for h in range(2):
                    last = nc.tensor.matmul(wide[j % 2][:, h * HALF:(h + 1) * HALF],
                                            queries_hi[u][:, j * P:(j + 1) * P],
                                            keys_hilo[u][:, h * HALF:(h + 1) * HALF], start=True, stop=True)
                last.then_inc(wide_made, 1)

            def transpose_max(p):
                pe.wait_ge(max_done, T * p + T)
                nc.tensor.matmul(misc[0:T, 0:P], chunk_max[:, :], identity, start=True,
                                 stop=True).then_inc(maxT_made, 1)

            def score_tile(b, u, i):
                if i == 0:
                    pe.wait_ge(score_stacks_moved, SCORE_MOVES * DMA * (b + 1))
                    pe.wait_ge(max_placed, DMA * (b + 1))
                for h in range(2):
                    half = slice(h * HALF, (h + 1) * HALF)
                    if i > 0:
                        pe.wait_ge(exp_done, 2 * T * b + 2 * i - 1 + h)
                    elif has_prior(b):
                        pe.wait_ge(exp_done, 2 * T * b - 1 + h)
                    nc.tensor.matmul(scores[:, half], keys_hilo[u][:, i * P:(i + 1) * P], queries_hi[u][:, half],
                                     start=True, stop=False)
                    nc.tensor.matmul(scores[:, half], keys_guard[u][:, i * P:(i + 1) * P], queries_lo[u][:, half],
                                     start=False, stop=True).then_inc(scores_made, 1)

            def weigh_values(b, u, i):
                tp, tt = divmod(i, PAIRS)
                v = values[u][:, (2 * tt + tp) * C:(2 * tt + tp + 1) * C]
                pe.wait_ge(exp_done, 2 * T * b + 2 * i + 2)
                if i == 0:
                    pe.wait_ge(values_done, b + 1)
                    if has_prior(b):
                        pe.wait_ge(attnT_done, b)
                nc.tensor.matmul(attn[0:C, :], v, probs[i % E_RING][:, 0:HALF], start=(i == 0), stop=(i == T - 1),
                                 skip_group_check=True)
                nc.tensor.matmul(attn[C:P, :], v, probs[i % E_RING][:, HALF:PIXELS], start=(i == 0),
                                 stop=(i == T - 1), skip_group_check=True).then_inc(pv_done, 1)

            def project_out(b):
                pe.wait_ge(attnT_done, b + 1)
                for tt in range(PAIRS):
                    last = nc.tensor.matmul(wide[1][:, tt * P:(tt + 1) * P], attn_T[:, tt * P:(tt + 1) * P], w_p2[:, :],
                                            start=True, stop=True)
                last.then_inc(y_made, 1)

            def denominators(b, u, last_image=False):
                if last_image:
                    pe.wait_ge(last_sum_done, T - 1)
                else:
                    pe.wait_ge(sum_done, (T - 1) * (b + 1))
                n = PIXELS // GROUPS
                for g in range(GROUPS):
                    last = nc.tensor.matmul(misc[g * ROWS:(g + 1) * ROWS, 0:n], ones[:, 0:ROWS],
                                            prob_sum[u][:, g * n:(g + 1) * n], start=True, stop=True)
                last.then_inc(sum_freed, 1)

            def turn_denominators(b):
                pe.wait_ge(den_copied, b + 1)
                for k in range(2):
                    last = nc.tensor.transpose(misc[:, k * P:(k + 1) * P], den_rows[:, k * P:(k + 1) * P], identity)
                last.then_inc(den_turned, 1)

            def prologue():
                pe.wait_ge(packed_loaded, DMA)
                transpose_x(0, 0, DMA)
                pe.wait_ge(blocks_done, 4)
                pe.wait_ge(beta_wide_done, 1)
                nc.tensor.matmul(attn[:, 0:1], w_qk[0:C, :], beta_col, start=True, stop=True)
                nc.tensor.matmul(attn[:, C:2 * C], beta_wide[:, :], w_v2[0:C, 0:C], start=True,
                                 stop=True).then_inc(biases_made, 1)
                group_means(0)
                group_variances(0)
                pe.wait_ge(var_done, 1)
                project_qk(0)
                project_v(0)
                pe.wait_ge(ones_done, 1)
                pe.wait_ge(values_done, 1)
                coefficients(0)
                max_chunk(0, 0, 0)
                max_chunk(0, 0, 1)
                pe.wait_ge(scaled_done, 1)
                transpose_x(1, 1, DMA)
                max_chunk(0, 0, 2)
                max_chunk(0, 0, 3)
                group_means(1)
                max_chunk(0, 0, 4)
                max_chunk(0, 0, 5)
                group_variances(1)
                max_chunk(0, 0, 6)
                max_chunk(0, 0, 7)
                pe.wait_ge(var_done, 2)
                pe.wait_ge(guard_done, 2)
                transpose_max(0)
                pe.wait_ge(maxT_done, 1)
                coefficients(1)

            def last_image(b, u):
                v = 1 - u
                score_tile(b, u, 0)
                weigh_values(b - 1, v, T - 1)
                for i in range(1, T):
                    score_tile(b, u, i)
                    weigh_values(b, u, i - 1)
                    if i == 1:
                        pe.wait_ge(maxT_done, b + 1)
                        denominators(b - 1, v)
                    if i == 3:
                        turn_denominators(b - 1)
                    if i == 4:
                        pe.wait_ge(y_mul_done, b - 1)
                        project_out(b - 1)
                weigh_values(b, u, T - 1)
                pe.wait_ge(inv_done, b)
                denominators(b, u, last_image=True)
                turn_denominators(b)
                pe.wait_ge(y_mul_done, b)
                project_out(b)

            def image(b, u, prior, nxt, after):
                if not nxt:
                    return last_image(b, u)
                p, s, v = b + 1, b + 2, 1 - u
                project_qk(p)
                score_tile(b, u, 0)
                if prior:
                    weigh_values(b - 1, v, T - 1)
                project_v(p)
                score_tile(b, u, 1)
                weigh_values(b, u, 0)
                if after:
                    pe.wait_ge(values_done, p + 1)
                    transpose_x(s, u, (b - u) * (DMA // 2) + 2 * DMA)

                score_tile(b, u, 2)
                weigh_values(b, u, 1)
                if after:
                    group_means(s)
                max_chunk(p, v, 0)

                score_tile(b, u, 3)
                max_chunk(p, v, 1)
                weigh_values(b, u, 2)
                max_chunk(p, v, 2)
                if after:
                    group_variances(s)

                score_tile(b, u, 4)
                max_chunk(p, v, 3)
                weigh_values(b, u, 3)
                if prior:
                    if after:
                        pe.wait_ge(var_done, s + 1)
                    else:
                        pe.wait_ge(values_done, p + 1)
                    denominators(b - 1, v)

                score_tile(b, u, 5)
                max_chunk(p, v, 4)
                weigh_values(b, u, 4)
                if prior:
                    turn_denominators(b - 1)
                max_chunk(p, v, 5)

                score_tile(b, u, 6)
                max_chunk(p, v, 6)
                weigh_values(b, u, 5)
                max_chunk(p, v, 7)

                score_tile(b, u, 7)
                if prior:
                    pe.wait_ge(inv_done, b)
                else:
                    pe.wait_ge(var_done, s + 1)
                transpose_max(p)
                weigh_values(b, u, 6)
                if prior:
                    project_out(b - 1)
                if after:
                    pe.wait_ge(maxT_done, p + 1)
                    coefficients(s)

            all_images(pe, prologue, image)


_WEIGHTS = ["wq", "wk", "wv", "wp"]


def kernel(**inputs):
    import numpy as _np
    import concourse.bacc as _bacc
    from concourse import mybir as _mybir
    from concourse.bass_utils import run_bass_kernel_spmd as _run

    nc = _bacc.Bacc("TRN2", target_bir_lowering=False, num_devices=1)
    of = {name.removeprefix("L0_conv_"): _np.ascontiguousarray(a) for name, a in inputs.items()}
    channels = of["x"].shape[-1]
    width = channels // 8
    group = (_np.arange(2 * channels) % channels) // width
    identity = _np.eye(2 * channels, dtype=_np.float32)
    group_mean = (group[:, None] == group[None, :]).astype(_np.float32) / _np.float32(4 * width)
    weights = _np.concatenate([of[name] for name in _WEIGHTS], axis=1)
    gamma2, beta2 = (_np.concatenate([of[name], of[name]])[:, None] for name in ("gamma", "beta"))
    bias_qk = _np.concatenate([of["bq"], of["bk"]])[:, None]
    of["packed"] = _np.concatenate([identity, group_mean, _np.concatenate([weights, weights]), gamma2, beta2,
                                    bias_qk], axis=1)
    arrays, args = {}, []
    for name in ("x", "beta", "bv", "bp", "packed"):
        arrays[f"in_{name}_dram"] = of[name]
        args.append(nc.dram_tensor(f"in_{name}_dram", of[name].shape, _mybir.dt.from_np(of[name].dtype),
                                   kind="ExternalInput").ap())
    shape = of["x"].shape
    out = nc.dram_tensor("out_0_dram", shape, _mybir.dt.float32, kind="ExternalOutput").ap()
    attention_block(nc, *args, out)
    r = _run(nc, [arrays], core_ids=[0])
    return r.results[0]["out_0_dram"]
```

```python
import numpy as np
import concourse.bass as bass
from concourse import mybir
from contextlib import ExitStack



def attention_block(nc, x, bp, beta, packed_in, out):
    fp32 = mybir.dt.float32
    fp32r = mybir.dt.float32r
    ALU = mybir.AluOpType
    ACT = mybir.ActivationFunctionType
    AX = mybir.AxisListType

    BATCH, HEIGHT, WIDTH, C = x.shape
    PIXELS = HEIGHT * WIDTH
    P = 128
    T = PIXELS // P
    HALF = PIXELS // 2
    PAIRS = T // 2
    GROUPS = 4
    ROWS = P // GROUPS
    SCALE = float(C) ** -0.5
    EPS = 1e-5
    E_RING = 4
    RSTD_AT = 3
    XN_HI_AT = 5
    DMA = 16
    MAX_MOVES = 4
    SCORE_MOVES = 2

    x_nat = x.rearrange("b h w c -> b (h w) c").rearrange("b (p t) c -> b p (t c)", p=P)
    out_nat = out.rearrange("b h w c -> b (h w) c").rearrange("b (p t) c -> b p (t c)", p=P)

    def in_all_partitions(v):
        return v.rearrange("(o c) -> o c", o=1).to_broadcast([P, C])

    ctx = ExitStack()
    with ctx:
        def sb(name, shape, dt=fp32):
            return ctx.enter_context(nc.sbuf_tensor(name, shape, dt))

        def ps(name, shape):
            return ctx.enter_context(nc.psum_tensor(name, shape, fp32))

        def sem(name):
            return ctx.enter_context(nc.semaphore(name))

        packed = sb("packed", [P, packed_in.shape[1]])
        identity = packed[:, 0:P]
        group_mean = packed[:, P:2 * P]
        w_qk = packed[:, 2 * P:3 * P]
        w_v_turned = packed[0:C, 3 * P:3 * P + C]
        w_p = packed[0:C, 3 * P + C:4 * P]
        gamma_col = packed[:, 4 * P:4 * P + 1]
        beta_col = packed[0:C, 4 * P + 1:4 * P + 2]
        bias_qk_in = packed[:, 4 * P + 2:4 * P + 3]
        bv_col = packed[0:C, 4 * P + 3:4 * P + 4]
        w_vp = sb("w_vp", [P, P])
        w_qk_hi = sb("w_qk_hi", [P, P], fp32r)
        w_qk_lo = sb("w_qk_lo", [P, P], fp32r)
        ones = sb("ones", [P, P])
        table_use = sb("table_use", [P, 1])
        beta_wide = sb("beta_wide", [C, P])
        bv_wide = sb("bv_wide", [C, P])
        bias_qk = sb("bias_qk", [P, 1])
        bp_all = sb("bp_all", [P, C])
        beta_all = sb("beta_all", [P, C])
        beta_bp = sb("beta_bp", [P, C])
        bias_out = sb("bias_out", [P, C])
        x_in = [sb(f"x_in{u}", [P, T * C]) for u in range(2)]
        x_T = sb("x_T", [P, HALF])
        xn_T = sb("xn_T", [P, HALF])
        xn_hi = sb("xn_hi", [P, HALF], fp32r)
        xn_lo = sb("xn_lo", [P, HALF], fp32r)
        bn6 = sb("bn6", [P, 6])
        part_means = bn6[:, 1:6:3]
        part_moments = bn6[:, 2:6:3]
        group_mean_of = sb("group_mean_of", [P, 1])
        mean_diff = sb("mean_diff", [P, 2])
        var_terms = sb("var_terms", [P, 4])
        var_eps = sb("var_eps", [P, 1])
        minus_half = sb("minus_half", [P, 1])
        rstd = sb("rstd", [P, 1])
        gain = sb("gain", [P, 1])
        diag = sb("diag", [C, 2, C])
        residual = sb("residual", [P, BATCH * T * C])
        centred = sb("centred", [P, T * C])
        scaled = sb("scaled", [P, T * C])
        hi = sb("hi", [P, PIXELS], fp32r)
        lo = sb("lo", [P, PIXELS], fp32r)
        queries_hi = [sb(f"queries_hi{u}", [P, PIXELS], fp32r) for u in range(2)]
        queries_lo = [sb(f"queries_lo{u}", [C + 1, PIXELS], fp32r) for u in range(2)]
        keys_hilo = [sb(f"keys_hilo{u}", [P, PIXELS], fp32r) for u in range(2)]
        keys_guard = [sb(f"keys_guard{u}", [C + 1, PIXELS], fp32r) for u in range(2)]
        values = [sb(f"values{u}", [P, T * C]) for u in range(2)]
        chunk_max = sb("chunk_max", [P, T])
        max_T = sb("max_T", [T, P], fp32r)
        probs = [sb(f"probs{k}", [P, PIXELS]) for k in range(E_RING)]
        prob_sum = [sb(f"prob_sum{u}", [P, PIXELS]) for u in range(2)]
        attn_T = sb("attn_T", [P, HALF])
        den_rows = sb("den_rows", [P, PIXELS // GROUPS])
        inv_den = sb("inv_den", [P, T])
        y_mul = sb("y_mul", [P, T * C])
        y_out = [sb(f"y_out{u}", [P, T * C]) for u in range(2)]

        scores = ps("scores", [P, PIXELS])
        wide = [ps(f"wide{k}", [P, PIXELS]) for k in range(2)]
        attn = ps("attn", [P, HALF])
        misc = ps("misc", [P, HALF])

        matrices_loaded = sem("matrices_loaded")
        packed_loaded = sem("packed_loaded")
        rows_loaded = sem("rows_loaded")
        x_loaded = [sem(f"x_loaded{u}") for u in range(2)]
        max_stacks_moved = sem("max_stacks_moved")
        score_stacks_moved = sem("score_stacks_moved")
        max_placed = sem("max_placed")
        y_freed = [sem(f"y_freed{u}") for u in range(2)]
        ones_done = sem("ones_done")
        guard_done = sem("guard_done")
        half_done = sem("half_done")
        zeros_done = sem("zeros_done")
        wide_done = sem("wide_done")
        w_vp_made = sem("w_vp_made")
        blocks_done = sem("blocks_done")
        w_qk_hi_done = sem("w_qk_hi_done")
        w_qk_lo_done = sem("w_qk_lo_done")
        biases_made = sem("biases_made")
        biases_done = sem("biases_done")
        bias_out_done = sem("bias_out_done")
        queries_stacked = sem("queries_stacked")
        keys_stacked = sem("keys_stacked")
        max_row_made = sem("max_row_made")
        max_row_done = sem("max_row_done")
        xT_made = sem("xT_made")
        xT_copied = sem("xT_copied")
        bn_done = sem("bn_done")
        moments_done = sem("moments_done")
        mean_made = sem("mean_made")
        mean_done = sem("mean_done")
        diff_done = sem("diff_done")
        diff2_done = sem("diff2_done")
        var_made = sem("var_made")
        var_done = sem("var_done")
        rstd_done = sem("rstd_done")
        gain_done = sem("gain_done")
        xnT_done = sem("xnT_done")
        xn_hi_done = sem("xn_hi_done")
        xn_lo_done = sem("xn_lo_done")
        diag_done = sem("diag_done")
        coef_made = sem("coef_made")
        centred_done = sem("centred_done")
        scaled_done = sem("scaled_done")
        residual_done = sem("residual_done")
        qk_made = sem("qk_made")
        hi_done = sem("hi_done")
        lo_done = sem("lo_done")
        v_made = sem("v_made")
        values_done = sem("values_done")
        wide_made = sem("wide_made")
        max_done = sem("max_done")
        maxT_made = sem("maxT_made")
        maxT_done = sem("maxT_done")
        scores_made = sem("scores_made")
        exp_done = sem("exp_done")
        pv_done = sem("pv_done")
        sum_done = sem("sum_done")
        last_sum_done = sem("last_sum_done")
        attnT_done = sem("attnT_done")
        y_made = sem("y_made")
        sum_freed = sem("sum_freed")
        den_copied = sem("den_copied")
        den_turned = sem("den_turned")
        inv_done = sem("inv_done")
        y_mul_done = sem("y_mul_done")
        y_done = sem("y_done")

        def per_channel(ap):
            return ap.unsqueeze(1).to_broadcast([P, T, C])

        def pixels(ap):
            return ap.rearrange("p (t c) -> p t c", t=T)

        FIRST, LOOP_FROM, LOOP_TO = 0, 1, BATCH - 4

        def all_images(eng, prologue, image):
            prologue()
            image(FIRST, FIRST % 2, prior=False, nxt=True, after=True)
            with eng.Fori(LOOP_FROM, LOOP_TO, 2) as b:
                image(b, LOOP_FROM % 2, prior=True, nxt=True, after=True)
                image(b + 1, (LOOP_FROM + 1) % 2, prior=True, nxt=True, after=True)
            image(BATCH - 3, (BATCH - 3) % 2, prior=True, nxt=True, after=True)
            image(BATCH - 2, (BATCH - 2) % 2, prior=True, nxt=True, after=False)
            image(BATCH - 1, (BATCH - 1) % 2, prior=True, nxt=False, after=False)

        def from_image(first, b):
            return not isinstance(b, int) or b >= first

        block = ctx.enter_context(nc.Block())

        @block.sync
        def _(sp):
            def load_x(b, u):
                sp.dma_start(x_in[u][:, :], x_nat[bass.ds(b, 1)].rearrange("o p f -> (o p) f")).then_inc(
                    x_loaded[u], DMA)

            def move(to, of, moved):
                sp.dma_start(to.bitcast(fp32), of.bitcast(fp32)).then_inc(moved, DMA)

            def stack_for_scores(p, u):
                sp.wait_ge(lo_done, 2 * p + 2)
                move(keys_guard[u][0:C, :], hi[C:P, :], score_stacks_moved)
                move(queries_lo[u][0:C, :], lo[0:C, :], score_stacks_moved)

            def stack_for_max(p, u):
                sp.wait_ge(hi_done, 2 * p + 2)
                move(queries_hi[u][0:C, :], hi[0:C, :], max_stacks_moved)
                move(queries_hi[u][C:P, :], hi[0:C, :], max_stacks_moved)
                move(keys_hilo[u][0:C, :], hi[C:P, :], max_stacks_moved)
                sp.wait_ge(lo_done, 2 * p + 2)
                move(keys_hilo[u][C:P, :], lo[C:P, :], max_stacks_moved)

            def place_max(p, u):
                sp.wait_ge(maxT_done, p)
                sp.dma_start(queries_lo[u][C:C + 1, :].bitcast(fp32).rearrange("o (t q) -> o t q", t=T),
                             max_T[:, :].bitcast(fp32)).then_inc(max_placed, DMA)

            def store(b, u):
                sp.wait_ge(y_done, b + 1)
                sp.dma_start(out_nat[bass.ds(b, 1)].rearrange("o p f -> (o p) f"), y_out[u][:, :]).then_inc(
                    y_freed[u], DMA)

            def prologue():
                load_x(0, 0)
                for part, loaded in ((slice(0, 2 * P), matrices_loaded), (slice(2 * P, None), packed_loaded)):
                    sp.dma_start(packed[:, part], packed_in[:, part]).then_inc(loaded, DMA)
                load_x(1, 1)
                sp.dma_start(bp_all[:, :], in_all_partitions(bp)).then_inc(rows_loaded, DMA)
                sp.dma_start(beta_all[:, :], in_all_partitions(beta)).then_inc(rows_loaded, DMA)
                stack_for_scores(0, 0)

            def image(b, u, prior, nxt, after):
                if nxt:
                    stack_for_max(b + 1, 1 - u)
                if not prior:
                    sp.wait_ge(centred_done, b + 1)
                    load_x(b + 2, u)
                if nxt:
                    stack_for_scores(b + 1, 1 - u)
                if not isinstance(b, int) or b + 3 < BATCH:
                    sp.wait_ge(centred_done, b + 2)
                    load_x(b + 3, 1 - u)
                if nxt:
                    place_max(b + 1, 1 - u)
                if prior:
                    store(b - 1, 1 - u)

            all_images(sp, prologue, image)
            store(BATCH - 1, (BATCH - 1) % 2)
            for u in range(2):
                sp.wait_ge(y_freed[u], DMA * (BATCH // 2 + 1))

        @block.gpsimd
        def _(pool):
            def rstd_of(s):
                pool.wait_ge(var_done, s + 1)
                if from_image(1, s):
                    pool.wait_ge(gain_done, s)
                nc.gpsimd.tensor_tensor(rstd[:, :], var_eps[:, :], minus_half[:, :], ALU.pow).then_inc(rstd_done, 1)

            def prologue():
                nc.gpsimd.memset(minus_half[:, :], -0.5).then_inc(half_done, 1)
                pool.wait_ge(half_done, 1)
                for u in range(2):
                    nc.gpsimd.memset(keys_guard[u][C:C + 1, :].bitcast(fp32), -1.0).then_inc(guard_done, 1)
                    pool.wait_ge(guard_done, u + 1)
                rstd_of(0)
                rstd_of(1)

            def image(b, u, prior, nxt, after):
                if not nxt:
                    return
                for i in range(1, T):
                    pool.wait_ge(exp_done, 2 * T * b + 2 * i + 2)
                    if i == 1:
                        pool.wait_ge(sum_freed, b + 1)
                        first = probs[0]
                    else:
                        pool.wait_ge(sum_done, (T - 1) * b + i - 1)
                        first = prob_sum[u]
                    nc.gpsimd.tensor_tensor(prob_sum[u][:, :], first[:, :], probs[i % E_RING][:, :],
                                            ALU.add).then_inc(sum_done, 1)
                    if i == RSTD_AT and after:
                        rstd_of(b + 2)

            all_images(pool, prologue, image)

        @block.scalar
        def _(act):
            def copy_xT(s):
                act.wait_ge(xT_made, s + 1)
                act.wait_ge(xnT_done, s)
                nc.scalar.copy(x_T[:, :], misc[:, :]).then_inc(xT_copied, 1)

            def round_xn(s):
                act.wait_ge(xnT_done, s + 1)
                act.wait_ge(qk_made, 2 * s)
                nc.scalar.copy(xn_hi[:, :], xn_T[:, :]).then_inc(xn_hi_done, 1)

            def copy_values(p, u, made_in):
                act.wait_ge(v_made, p + 1)
                if from_image(2, p):
                    act.wait_ge(pv_done, T * (p - 1))
                nc.scalar.copy(values[u][:, :], made_in[:, :]).then_inc(values_done, 1)

            def split_hi(p):
                for h in range(2):
                    act.wait_ge(qk_made, 2 * p + h + 1)
                    if h == 0 and from_image(1, p):
                        if from_image(2, p):
                            act.wait_ge(max_stacks_moved, MAX_MOVES * DMA * (p - 1))
                        act.wait_ge(score_stacks_moved, SCORE_MOVES * DMA * p)
                    nc.scalar.activation(hi[:, h * HALF:(h + 1) * HALF], wide[0][:, h * HALF:(h + 1) * HALF],
                                         ACT.Identity, bias=bias_qk[:, 0:1]).then_inc(hi_done, 1)

            def copy_attn(b):
                act.wait_ge(pv_done, T * b + T)
                if from_image(1, b):
                    act.wait_ge(y_made, b)
                nc.scalar.copy(attn_T[:, :], attn[:, :]).then_inc(attnT_done, 1)

            def prologue():
                act.wait_ge(ones_done, 1)
                nc.scalar.activation(table_use[:, :], ones[:, 0:1], ACT.Exp)
                act.wait_ge(biases_done, 2)
                split_hi(0)
                act.wait_ge(hi_done, 2)
                for half in (slice(0, C), slice(C, P)):
                    nc.scalar.copy(queries_hi[0][half, :], hi[0:C, :]).then_inc(queries_stacked, 1)
                copy_values(0, 0, attn)
                copy_values(1, 1, attn)
                for h in range(2):
                    half = slice(h * HALF, (h + 1) * HALF)
                    act.wait_ge(max_row_made, h + 1)
                    nc.scalar.copy(queries_lo[0][C:C + 1, half], scores[C:C + 1, half]).then_inc(max_row_done, 1)

            def image(b, u, prior, nxt, after):
                if nxt:
                    split_hi(b + 1)
                for i in range(T):
                    for h in range(2):
                        act.wait_ge(scores_made, 2 * T * b + 2 * i + h + 1)
                        if i >= E_RING:
                            act.wait_ge(pv_done, T * b + i - E_RING + 1)
                            summed = max(i - E_RING, 1)
                            if nxt:
                                act.wait_ge(sum_done, (T - 1) * b + summed)
                            else:
                                act.wait_ge(last_sum_done, summed)
                        elif prior:
                            act.wait_ge(pv_done, T * b + i - E_RING + 1)
                            act.wait_ge(sum_done, (T - 1) * b + i - E_RING + 1)
                        nc.scalar.activation(probs[i % E_RING][:, h * HALF:(h + 1) * HALF],
                                             scores[:, h * HALF:(h + 1) * HALF], ACT.Exp,
                                             scale=SCALE).then_inc(exp_done, 1)
                    if i == 0 and prior:
                        copy_attn(b - 1)
                        if nxt:
                            copy_values(b + 1, 1 - u, misc)
                    if i == (1 if prior else 3) and after:
                        copy_xT(b + 2)
                    if i == XN_HI_AT and after:
                        round_xn(b + 2)

            all_images(act, prologue, image)
            copy_attn(BATCH - 1)

        @block.vector
        def _(dve):
            def part_statistics(s, turned=None):
                if turned is None:
                    dve.wait_ge(xT_copied, s - 1)
                    turned = x_T[:, :]
                else:
                    dve.wait_ge(xT_made, s + 1)
                if from_image(1, s):
                    dve.wait_ge(var_made, s)
                nc.vector.bn_stats(bn6[:, :], turned).then_inc(bn_done, 1)
                dve.wait_ge(bn_done, s + 1)
                nc.vector.tensor_scalar(var_terms[:, 2:4], part_moments, 2.0 / HALF, EPS, ALU.mult,
                                        ALU.add).then_inc(moments_done, 1)

            def mean_differences(s):
                dve.wait_ge(mean_made, s + 1)
                nc.vector.reduce_sum(group_mean_of[:, :], misc[:, 0:2], AX.X).then_inc(mean_done, 1)
                dve.wait_ge(mean_done, s + 1)
                nc.vector.tensor_scalar(mean_diff[:, :], part_means, group_mean_of[:, 0:1], None,
                                        ALU.subtract).then_inc(diff_done, 1)
                dve.wait_ge(diff_done, s + 1)
                nc.vector.tensor_tensor(var_terms[:, 0:2], mean_diff[:, :], mean_diff[:, :],
                                        ALU.mult).then_inc(diff2_done, 1)

            def variance(s):
                dve.wait_ge(var_made, s + 1)
                nc.vector.reduce_sum(var_eps[:, :], misc[:, 0:4], AX.X).then_inc(var_done, 1)

            def normalise(s, turned=None):
                dve.wait_ge(rstd_done, s + 1)
                nc.vector.tensor_tensor(gain[:, :], rstd[:, :], gamma_col[:, :], ALU.mult).then_inc(gain_done, 1)
                dve.wait_ge(gain_done, s + 1)
                if from_image(1, s):
                    dve.wait_ge(v_made, s)
                nc.vector.tensor_scalar(xn_T[:, :], x_T[:, :] if turned is None else turned, group_mean_of[:, 0:1],
                                        gain[:, 0:1], ALU.subtract, ALU.mult).then_inc(xnT_done, 1)
                if from_image(1, s):
                    dve.wait_ge(coef_made, s)
                nc.vector.tensor_scalar(diag[:, 0, :], identity[0:C, 0:C], gain[0:C, 0:1], None, ALU.mult)
                nc.vector.tensor_scalar(diag[:, 1, :], identity[0:C, 0:C], group_mean_of[0:C, 0:1], None,
                                        ALU.mult).then_inc(diag_done, 1)

            def split_xn(s):
                dve.wait_ge(xn_hi_done, s - 1)
                nc.vector.tensor_tensor(xn_lo[:, :], xn_T[:, :], xn_hi[:, :].bitcast(fp32),
                                        ALU.subtract).then_inc(xn_lo_done, 1)

            def residual_of(s, u, at=0):
                dve.wait_ge(coef_made, s + 1)
                nc.vector.tensor_tensor(pixels(centred[:, :]), pixels(x_in[u][:, :]),
                                        per_channel(misc[:, at + C:at + 2 * C]), ALU.subtract).then_inc(centred_done, 1)
                dve.wait_ge(centred_done, s + 1)
                nc.vector.tensor_tensor(pixels(scaled[:, :]), pixels(centred[:, :]), per_channel(misc[:, at:at + C]),
                                        ALU.mult).then_inc(scaled_done, 1)
                dve.wait_ge(scaled_done, s + 1)
                nc.vector.tensor_tensor(pixels(residual[:, bass.ds(s * (T * C), T * C)]), pixels(scaled[:, :]),
                                        per_channel(bias_out[:, :]), ALU.add).then_inc(residual_done, 1)

            def split_lo_half(p, h):
                half = slice(h * HALF, (h + 1) * HALF)
                dve.wait_ge(hi_done, 2 * p + h + 1)
                if h == 0 and from_image(1, p):
                    if from_image(2, p):
                        dve.wait_ge(max_stacks_moved, MAX_MOVES * DMA * (p - 1))
                    dve.wait_ge(score_stacks_moved, SCORE_MOVES * DMA * p)
                nc.vector.scalar_tensor_tensor(lo[:, half], wide[0][:, half], bias_qk[:, 0:1],
                                               hi[:, half].bitcast(fp32), ALU.add,
                                               ALU.subtract).then_inc(lo_done, 1)

            def reduce_chunk(p, j):
                dve.wait_ge(wide_made, T * p + j + 1)
                if j == 0 and from_image(2, p):
                    dve.wait_ge(maxT_made, p - 1)
                elif j == 0 and from_image(1, p):
                    dve.wait_ge(max_row_made, 2)
                nc.vector.reduce_max(chunk_max[:, j:j + 1], wide[j % 2][:, :], AX.X).then_inc(max_done, 1)

            def copy_maxT(p):
                dve.wait_ge(maxT_made, p)
                if from_image(2, p):
                    dve.wait_ge(max_placed, DMA * (p - 1))
                nc.vector.tensor_copy(max_T[:, :], misc[0:T, 0:P]).then_inc(maxT_done, 1)

            def copy_den(b):
                dve.wait_ge(sum_freed, b + 3)
                nc.vector.tensor_copy(den_rows[:, :], misc[:, 0:PIXELS // GROUPS]).then_inc(den_copied, 1)

            def invert(b):
                dve.wait_ge(den_turned, b + 1)
                turned = misc[:, 0:2 * P:ROWS].rearrange("p (k a c) -> p k a c", k=2, a=2)
                nc.vector.reciprocal(inv_den[:, :].rearrange("p (c k a) -> p k a c", c=2, k=2),
                                     turned).then_inc(inv_done, 1)

            def finish(b, u):
                dve.wait_ge(inv_done, b + 1)
                dve.wait_ge(y_made, b + 1)
                nc.vector.tensor_tensor(pixels(y_mul[:, :]), pixels(wide[1][:, 0:HALF]),
                                        inv_den[:, :].unsqueeze(2).to_broadcast([P, T, C]),
                                        ALU.mult).then_inc(y_mul_done, 1)
                dve.wait_ge(y_mul_done, b + 2)
                dve.wait_ge(y_freed[u], (b - u) * (DMA // 2) + DMA)
                nc.vector.tensor_tensor(y_out[u][:, :], y_mul[:, :], residual[:, bass.ds(b * (T * C), T * C)],
                                        ALU.add).then_inc(y_done, 1)

            def sum_probs(b, u, i):
                dve.wait_ge(exp_done, 2 * T * b + 2 * i + 2)
                if i == 1:
                    dve.wait_ge(sum_freed, b + 1)
                    first = probs[0]
                else:
                    dve.wait_ge(last_sum_done, i - 1)
                    first = prob_sum[u]
                nc.vector.tensor_tensor(prob_sum[u][:, :], first[:, :], probs[i % E_RING][:, :],
                                        ALU.add).then_inc(last_sum_done, 1)

            def prologue():
                nc.vector.memset(ones[:, :], 1.0).then_inc(ones_done, 1)
                nc.vector.memset(w_vp[:, :], 0.0).then_inc(zeros_done, 1)
                nc.vector.memset(mean_diff[:, :], 0.0).then_inc(sum_freed, 2)
                nc.vector.memset(y_mul[:, 0:1], 0.0).then_inc(y_mul_done, 1)
                for u in range(2):
                    nc.vector.memset(y_out[u][:, 0:1], 0.0).then_inc(y_freed[u], DMA)
                dve.wait_ge(packed_loaded, DMA)
                nc.vector.tensor_copy(beta_wide[:, :], beta_col.to_broadcast([C, P])).then_inc(wide_done, 1)
                nc.vector.tensor_copy(bv_wide[:, :], bv_col.to_broadcast([C, P])).then_inc(wide_done, 1)
                nc.vector.tensor_copy(w_qk_hi[:, :], w_qk).then_inc(w_qk_hi_done, 1)
                part_statistics(0, wide[1][:, 0:HALF])
                dve.wait_ge(w_vp_made, 1)
                dve.wait_ge(zeros_done, 1)
                for rows in (slice(0, C), slice(C, P)):
                    nc.vector.tensor_copy(w_vp[rows, rows], attn[rows, 0:C]).then_inc(blocks_done, 1)
                mean_differences(0)
                variance(0)
                dve.wait_ge(biases_made, 1)
                nc.vector.tensor_tensor(bias_qk[:, :], attn[:, 2 * C:2 * C + 1], bias_qk_in,
                                        ALU.add).then_inc(biases_done, 1)
                dve.wait_ge(rows_loaded, 2 * DMA)
                nc.vector.tensor_tensor(beta_bp[:, :], beta_all[:, :], bp_all[:, :], ALU.add).then_inc(biases_done, 1)
                normalise(0, wide[1][:, 0:HALF])
                dve.wait_ge(biases_done, 2)
                nc.vector.tensor_tensor(bias_out[:, :], attn[:, C:2 * C], beta_bp[:, :],
                                        ALU.add).then_inc(bias_out_done, 1)
                dve.wait_ge(w_qk_hi_done, 1)
                nc.vector.tensor_tensor(w_qk_lo[:, :], w_qk, w_qk_hi[:, :].bitcast(fp32),
                                        ALU.subtract).then_inc(w_qk_lo_done, 1)
                part_statistics(1, scores[:, 0:HALF])
                mean_differences(1)
                split_lo_half(0, 0)
                variance(1)
                split_lo_half(0, 1)
                dve.wait_ge(lo_done, 2)
                nc.vector.tensor_copy(keys_hilo[0][C:P, :], lo[C:P, :]).then_inc(keys_stacked, 1)
                nc.vector.tensor_copy(keys_hilo[0][0:C, :], hi[C:P, :]).then_inc(keys_stacked, 1)
                normalise(1, scores[:, 0:HALF])
                for j in range(T):
                    reduce_chunk(0, j)

            def image(b, u, prior, nxt, after):
                p, s, v = b + 1, b + 2, 1 - u
                if not nxt:
                    copy_den(b - 1)
                    invert(b - 1)
                    for i in range(1, T):
                        sum_probs(b, u, i)
                        if i == 2:
                            finish(b - 1, v)
                    return
                for h in range(2):
                    split_lo_half(p, h)
                if not prior:
                    dve.wait_ge(bias_out_done, 1)
                    residual_of(b, u)
                    residual_of(p, v, 2 * C)
                if after and prior:
                    part_statistics(s)
                reduce_chunk(p, 0)
                if not prior:
                    part_statistics(s)
                elif after:
                    mean_differences(s)
                reduce_chunk(p, 1)
                if not prior:
                    mean_differences(s)
                reduce_chunk(p, 2)
                if after and prior:
                    variance(s)
                reduce_chunk(p, 3)
                if not prior:
                    variance(s)
                elif after:
                    normalise(s)
                reduce_chunk(p, 4)
                if prior:
                    copy_den(b - 1)
                else:
                    normalise(s)
                reduce_chunk(p, 5)
                reduce_chunk(p, 6)
                if prior:
                    invert(b - 1)
                reduce_chunk(p, 7)
                copy_maxT(p)
                if after:
                    split_xn(s)
                if prior:
                    finish(b - 1, v)
                if after:
                    residual_of(s, u)

            all_images(dve, prologue, image)
            copy_den(BATCH - 1)
            invert(BATCH - 1)
            finish(BATCH - 1, (BATCH - 1) % 2)

        @block.tensor
        def _(pe):
            def transpose_x(s, u, loads, to=misc):
                pe.wait_ge(x_loaded[u], loads)
                for tt in range(PAIRS):
                    last = nc.tensor.transpose(to[:, tt * P:(tt + 1) * P], x_in[u][:, tt * P:(tt + 1) * P],
                                               identity)
                last.then_inc(xT_made, 1)

            def group_means(s):
                pe.wait_ge(bn_done, s + 1)
                nc.tensor.matmul(misc[:, 0:2], group_mean, part_means, start=True,
                                 stop=True).then_inc(mean_made, 1)

            def group_variances(s):
                pe.wait_ge(moments_done, s + 1)
                pe.wait_ge(diff2_done, s + 1)
                nc.tensor.matmul(misc[:, 0:4], group_mean, var_terms[:, :], start=True,
                                 stop=True).then_inc(var_made, 1)

            def coefficients(s, at=0):
                pe.wait_ge(diag_done, s + 1)
                nc.tensor.matmul(misc[:, at:at + 2 * C], ones[0:C, :], diag[:, :, :].rearrange("p a c -> p (a c)"),
                                 start=True, stop=True).then_inc(coef_made, 1)

            def project_qk_half(p, tp):
                rows, half = slice(tp * C, (tp + 1) * C), slice(tp * HALF, (tp + 1) * HALF)
                if not from_image(2, p):
                    pe.wait_ge(xnT_done, p + 1)
                    nc.tensor.matmul(wide[0][:, half], w_qk[rows, :], xn_T[rows, :], start=True,
                                     stop=True).then_inc(qk_made, 1)
                    return
                if tp == 0:
                    pe.wait_ge(xn_lo_done, p - 1)
                nc.tensor.matmul(wide[0][:, half], w_qk_hi[rows, :], xn_hi[rows, :], start=True, stop=False)
                nc.tensor.matmul(wide[0][:, half], w_qk_lo[rows, :], xn_hi[rows, :], start=False, stop=False)
                nc.tensor.matmul(wide[0][:, half], w_qk_hi[rows, :], xn_lo[rows, :], start=False,
                                 stop=True).then_inc(qk_made, 1)

            def project_v(p, to=misc):
                for tt in range(PAIRS):
                    last = nc.tensor.matmul(to[:, tt * P:(tt + 1) * P], xn_T[:, tt * P:(tt + 1) * P], w_vp[:, :],
                                            start=True, stop=True)
                last.then_inc(v_made, 1)

            def max_chunk(p, u, j):
                if j == 0:
                    if from_image(1, p):
                        pe.wait_ge(max_stacks_moved, MAX_MOVES * DMA * p)
                    else:
                        pe.wait_ge(queries_stacked, 2)
                        pe.wait_ge(keys_stacked, 2)
                    pe.wait_ge(lo_done, 2 * p + 2)
                elif j == 1:
                    if from_image(2, p):
                        pe.wait_ge(y_mul_done, p - 1)
                    elif not from_image(1, p):
                        pe.wait_ge(xnT_done, 1)
                else:
                    pe.wait_ge(max_done, T * p + j - 1)
                for h in range(2):
                    last = nc.tensor.matmul(wide[j % 2][:, h * HALF:(h + 1) * HALF],
                                            queries_hi[u][:, j * P:(j + 1) * P],
                                            keys_hilo[u][:, h * HALF:(h + 1) * HALF], start=True, stop=True)
                last.then_inc(wide_made, 1)

            def transpose_max(p):
                pe.wait_ge(max_done, T * p + T)
                nc.tensor.matmul(misc[0:T, 0:P], chunk_max[:, :], identity, start=True,
                                 stop=True).then_inc(maxT_made, 1)

            def turn_first_max(j):
                pe.wait_ge(max_done, j + 1)
                last = nc.tensor.matmul(scores[C:C + 1, j * P:(j + 1) * P], chunk_max[:, j:j + 1], identity,
                                        start=True, stop=True)
                if j % PAIRS == PAIRS - 1:
                    last.then_inc(max_row_made, 1)

            def score_tile(b, u, i):
                first_image = not from_image(1, b)
                if i == 0:
                    pe.wait_ge(score_stacks_moved, SCORE_MOVES * DMA * (b + 1))
                    if first_image:
                        pe.wait_ge(guard_done, 2)
                    else:
                        pe.wait_ge(max_placed, DMA * b)
                for h in range(2):
                    half = slice(h * HALF, (h + 1) * HALF)
                    if i > 0:
                        pe.wait_ge(exp_done, 2 * T * b + 2 * i - 1 + h)
                    elif first_image:
                        pe.wait_ge(max_row_done, h + 1)
                    else:
                        pe.wait_ge(exp_done, 2 * T * b - 1 + h)
                    nc.tensor.matmul(scores[:, half], keys_hilo[u][:, i * P:(i + 1) * P], queries_hi[u][:, half],
                                     start=True, stop=False)
                    nc.tensor.matmul(scores[:, half], keys_guard[u][:, i * P:(i + 1) * P], queries_lo[u][:, half],
                                     start=False, stop=True).then_inc(scores_made, 1)

            def weigh_values(b, u, i):
                tp, tt = divmod(i, PAIRS)
                v = values[u][:, (2 * tt + tp) * C:(2 * tt + tp + 1) * C]
                pe.wait_ge(exp_done, 2 * T * b + 2 * i + 2)
                if i == 0:
                    pe.wait_ge(values_done, b + 1)
                    if from_image(1, b):
                        pe.wait_ge(attnT_done, b)
                nc.tensor.matmul(attn[0:C, :], v, probs[i % E_RING][:, 0:HALF], start=(i == 0), stop=(i == T - 1),
                                 skip_group_check=True)
                nc.tensor.matmul(attn[C:P, :], v, probs[i % E_RING][:, HALF:PIXELS], start=(i == 0),
                                 stop=(i == T - 1), skip_group_check=True).then_inc(pv_done, 1)

            def turn_outcome(b):
                pe.wait_ge(attnT_done, b + 1)
                for tt in range(PAIRS):
                    last = nc.tensor.transpose(wide[1][:, tt * P:(tt + 1) * P], attn_T[:, tt * P:(tt + 1) * P],
                                               identity)
                last.then_inc(y_made, 1)

            def denominators(b, u, last_image=False):
                if last_image:
                    pe.wait_ge(last_sum_done, T - 1)
                else:
                    pe.wait_ge(sum_done, (T - 1) * (b + 1))
                n = PIXELS // GROUPS
                for g in range(GROUPS):
                    last = nc.tensor.matmul(misc[g * ROWS:(g + 1) * ROWS, 0:n], ones[:, 0:ROWS],
                                            prob_sum[u][:, g * n:(g + 1) * n], start=True, stop=True)
                last.then_inc(sum_freed, 1)

            def turn_denominators(b):
                pe.wait_ge(den_copied, b + 1)
                for k in range(2):
                    last = nc.tensor.transpose(misc[:, k * P:(k + 1) * P], den_rows[:, k * P:(k + 1) * P], identity)
                last.then_inc(den_turned, 1)

            def keep_warm(to, products):
                for _ in range(products):
                    nc.tensor.matmul(to[:, 0:P], ones[:, :], ones[:, :], start=True, stop=True)

            def prologue():
                pe.wait_ge(ones_done, 1)
                keep_warm(misc, 6)
                pe.wait_ge(matrices_loaded, DMA)
                transpose_x(0, 0, DMA, wide[1])
                pe.wait_ge(packed_loaded, DMA)
                for rows in (slice(0, C), slice(C, P)):
                    last = nc.tensor.matmul(attn[rows, 0:C], w_v_turned, w_p, start=True, stop=True)
                last.then_inc(w_vp_made, 1)
                keep_warm(misc, 2)
                group_means(0)
                transpose_x(1, 1, DMA, scores)
                keep_warm(scores[:, HALF:], 1)
                group_variances(0)
                pe.wait_ge(blocks_done, 2)
                pe.wait_ge(wide_done, 2)
                nc.tensor.matmul(attn[:, 2 * C:2 * C + 1], w_qk[0:C, :], beta_col, start=True, stop=True)
                nc.tensor.matmul(attn[:, C:2 * C], beta_wide[:, :], w_vp[0:C, 0:C], start=True, stop=False)
                nc.tensor.matmul(attn[:, C:2 * C], bv_wide[:, :], w_p, start=False, stop=True).then_inc(biases_made, 1)
                keep_warm(scores[:, HALF:], 3)
                project_qk_half(0, 0)
                group_means(1)
                project_qk_half(0, 1)
                group_variances(1)
                pe.wait_ge(bias_out_done, 1)
                project_v(0, attn)
                pe.wait_ge(var_done, 2)
                coefficients(0)
                keep_warm(scores[:, HALF:], 3)
                max_chunk(0, 0, 0)
                max_chunk(0, 0, 1)
                coefficients(1, 2 * C)
                pe.wait_ge(values_done, 1)
                for j in range(2, T):
                    keep_warm(attn, 1)
                    turn_first_max(j - 2)
                    max_chunk(0, 0, j)
                project_v(1, attn)
                turn_first_max(T - 2)
                project_qk_half(1, 0)
                turn_first_max(T - 1)
                project_qk_half(1, 1)
                pe.wait_ge(w_qk_lo_done, 1)

            def last_image(b, u):
                v = 1 - u
                weigh_values(b - 1, v, T - 1)
                pe.wait_ge(maxT_done, b)
                denominators(b - 1, v)
                score_tile(b, u, 0)
                turn_denominators(b - 1)
                for i in range(1, T):
                    score_tile(b, u, i)
                    weigh_values(b, u, i - 1)
                    if i == 1:
                        pe.wait_ge(y_mul_done, b)
                        turn_outcome(b - 1)
                weigh_values(b, u, T - 1)
                pe.wait_ge(inv_done, b)
                denominators(b, u, last_image=True)
                pe.wait_ge(y_mul_done, b + 1)
                turn_outcome(b)
                turn_denominators(b)

            def image(b, u, prior, nxt, after):
                if not nxt:
                    return last_image(b, u)
                p, s, v = b + 1, b + 2, 1 - u
                if prior:
                    project_qk_half(p, 0)
                    project_qk_half(p, 1)
                score_tile(b, u, 0)
                if prior:
                    weigh_values(b - 1, v, T - 1)
                    pe.wait_ge(scaled_done, p + 1)
                    project_v(p)
                score_tile(b, u, 1)
                if after and prior:
                    pe.wait_ge(values_done, p + 1)
                    transpose_x(s, u, (b - u) * (DMA // 2) + 2 * DMA)
                score_tile(b, u, 2)
                weigh_values(b, u, 0)
                weigh_values(b, u, 1)
                if prior:
                    max_chunk(p, v, 0)
                    if after:
                        group_means(s)
                    score_tile(b, u, 3)
                else:
                    score_tile(b, u, 3)
                    max_chunk(p, v, 0)
                    pe.wait_ge(scaled_done, 2)
                    transpose_x(s, u, 2 * DMA)
                max_chunk(p, v, 1)
                score_tile(b, u, 4)
                if not prior:
                    group_means(s)
                max_chunk(p, v, 2)
                if after and prior:
                    group_variances(s)
                weigh_values(b, u, 2)
                max_chunk(p, v, 3)
                if not prior:
                    group_variances(s)
                weigh_values(b, u, 3)

                max_chunk(p, v, 4)
                score_tile(b, u, 5)
                if prior:
                    if after:
                        pe.wait_ge(var_done, s + 1)
                    else:
                        pe.wait_ge(values_done, p + 1)
                    denominators(b - 1, v)
                max_chunk(p, v, 5)
                score_tile(b, u, 6)
                max_chunk(p, v, 6)
                weigh_values(b, u, 4)
                if prior:
                    turn_denominators(b - 1)
                max_chunk(p, v, 7)
                score_tile(b, u, 7)
                weigh_values(b, u, 5)
                if prior:
                    pe.wait_ge(inv_done, b)
                else:
                    pe.wait_ge(var_done, s + 1)
                transpose_max(p)
                weigh_values(b, u, 6)
                if prior:
                    turn_outcome(b - 1)
                if after:
                    pe.wait_ge(maxT_done, p)
                    coefficients(s)

            all_images(pe, prologue, image)


def kernel(**inputs):
    import numpy as _np
    import concourse.bacc as _bacc
    from concourse import mybir as _mybir
    from concourse.bass_utils import run_bass_kernel_spmd as _run

    nc = _bacc.Bacc("TRN2", target_bir_lowering=False, num_devices=1)
    of = {name.removeprefix("L0_conv_"): _np.ascontiguousarray(a) for name, a in inputs.items()}
    channels = of["x"].shape[-1]
    width = channels // 8
    group = (_np.arange(2 * channels) % channels) // width
    identity = _np.eye(2 * channels, dtype=_np.float32)
    group_mean = (group[:, None] == group[None, :]).astype(_np.float32) / _np.float32(4 * width)
    weights = _np.concatenate([of["wq"], of["wk"], of["wv"].T, of["wp"]], axis=1)
    gamma2, beta2, bv2 = (_np.concatenate([of[name], of[name]])[:, None] for name in ("gamma", "beta", "bv"))
    bias_qk = _np.concatenate([of["bq"], of["bk"]])[:, None]
    of["packed"] = _np.concatenate([identity, group_mean, _np.concatenate([weights, weights]), gamma2, beta2,
                                    bias_qk, bv2], axis=1)
    arrays, args = {}, []
    for name in ("x", "bp", "beta", "packed"):
        arrays[f"in_{name}_dram"] = of[name]
        args.append(nc.dram_tensor(f"in_{name}_dram", of[name].shape, _mybir.dt.from_np(of[name].dtype),
                                   kind="ExternalInput").ap())
    shape = of["x"].shape
    out = nc.dram_tensor("out_0_dram", shape, _mybir.dt.float32, kind="ExternalOutput").ap()
    attention_block(nc, *args, out)
    r = _run(nc, [arrays], core_ids=[0])
    return r.results[0]["out_0_dram"]
```
